# Optimizing a Trainium2 kernel written in Bass

```python
import numpy as np
import jax
import jax.numpy as jnp

def _softmax(x, axis=-1):
    return jax.nn.softmax(x, axis=axis)

def _gelu(x):
    return jax.nn.gelu(x, approximate=True)

def _silu(x):
    return jax.nn.silu(x)

def _sigmoid(x):
    return jax.nn.sigmoid(x)

def _layernorm(x, axis=-1, eps=1e-05):
    m = jnp.mean(x, axis=axis, keepdims=True)
    v = jnp.var(x, axis=axis, keepdims=True)
    return (x - m) / jnp.sqrt(v + eps)

def _scatter_add(tgt, idx, src, axis=0):
    return tgt.at[idx].add(src)

def _segment_sum(src, seg, n):
    return jax.ops.segment_sum(src, seg, n)
kernel_name = 'mk_gnn_ffn_d1_gnn_r8_99539a'

def setup_inputs(seed: int=0):
    np.random.seed(seed)
    _w = jnp.asarray

    def _rec_inputs():
        import jax
        import jax.numpy as jnp
        _gk = jax.random.key(seed)
        x = -0.0002117 + 1 * jax.random.normal(jax.random.fold_in(_gk, 1), (12500, 256), jnp.float32)
        src = jax.random.randint(jax.random.fold_in(_gk, 2), (200000,), 0, 12500, jnp.int32)
        dst = jax.random.randint(jax.random.fold_in(_gk, 3), (200000,), 0, 12500, jnp.int32)
        _o = jnp.argsort(dst, stable=True)
        src = src[_o]
        dst = dst[_o]
        return (x, src, dst)
    x, src, dst = _rec_inputs()

    def _L0_gnn_setup():
        import jax, jax.numpy as jnp
        import numpy as np
        N_NODES = 12500
        N_EDGES = 400000
        IN_FEATS = 256
        OUT_FEATS = 256
        key = jax.random.key(seed)
        k1, k2, k3, k4 = jax.random.split(key, 4)
        x = jax.random.normal(k1, (N_NODES, IN_FEATS), dtype=jnp.float32)
        edge_index = jax.random.randint(k2, (2, N_EDGES), 0, N_NODES, dtype=jnp.int64)
        bound = 1.0 / np.sqrt(2 * IN_FEATS)
        W = jax.random.uniform(k3, (OUT_FEATS, 2 * IN_FEATS), minval=-bound, maxval=bound, dtype=jnp.float32)
        b = jax.random.uniform(k4, (OUT_FEATS,), minval=-bound, maxval=bound, dtype=jnp.float32)
        return {'x': x, 'edge_index': edge_index, 'W': W, 'b': b}
    _L0_gnn_all = _L0_gnn_setup()
    _L0_gnn_in = {k: v for k, v in _L0_gnn_all.items() if k in ('W', 'b')}
    del _L0_gnn_all

    def _L0_ffn_setup():
        import jax, jax.numpy as jnp
        import numpy as np
        NUM_EXPERTS = 8
        TOP_K = 2
        B, S, D = (8, 1024, 256)

        def _moe(tokens, router_w, w1, b1, w2, b2):
            N = tokens.shape[0]
            E = router_w.shape[0]
            logits = tokens.astype(jnp.float32) @ router_w.astype(jnp.float32).T
            probs = jax.nn.softmax(logits, axis=-1)
            rw, re = jax.lax.top_k(probs, TOP_K)
            if TOP_K > 1:
                rw = rw / jnp.maximum(rw.sum(-1, keepdims=True), 1e-12)
            rw = rw.astype(tokens.dtype)
            combine = jnp.zeros((N, E), tokens.dtype).at[jnp.arange(N)[:, None], re].set(rw)
            out = tokens
            for e in range(E):
                h = jax.nn.gelu(tokens @ w1[e] + b1[e], approximate=False)
                y = h @ w2[e] + b2[e]
                out = out + combine[:, e:e + 1] * y
            return out
        key = jax.random.key(seed)
        ks = jax.random.split(key, 4)
        scale = 1.0 / np.sqrt(D).astype(np.float32)
        return {'input_embeddings': jax.random.normal(ks[0], (B, S, D), jnp.float32), 'router_w': jax.random.normal(ks[1], (NUM_EXPERTS, D), jnp.float32) * scale, 'w1': jax.random.normal(ks[2], (NUM_EXPERTS, D, D), jnp.float32) * scale, 'b1': jnp.zeros((NUM_EXPERTS, D), jnp.float32), 'w2': jax.random.normal(ks[3], (NUM_EXPERTS, D, D), jnp.float32) * scale, 'b2': jnp.zeros((NUM_EXPERTS, D), jnp.float32)}
    _L0_ffn_all = _L0_ffn_setup()
    _L0_ffn_in = {k: v for k, v in _L0_ffn_all.items() if k in ('router_w', 'w1', 'b1', 'w2', 'b2')}
    del _L0_ffn_all
    return {'x': x, 'src': src, 'dst': dst, 'L0_gnn_W': _L0_gnn_in['W'], 'L0_gnn_b': _L0_gnn_in['b'], 'L0_ffn_router_w': _L0_ffn_in['router_w'], 'L0_ffn_w1': _L0_ffn_in['w1'], 'L0_ffn_b1': _L0_ffn_in['b1'], 'L0_ffn_w2': _L0_ffn_in['w2'], 'L0_ffn_b2': _L0_ffn_in['b2']}

def reference(x, src, dst, L0_gnn_W, L0_gnn_b, L0_ffn_router_w, L0_ffn_w1, L0_ffn_b1, L0_ffn_w2, L0_ffn_b2):
    import jax
    import jax.numpy as jnp

    def _L0_gnn_ref(x, edge_index, W, b):
        import jax, jax.numpy as jnp
        import numpy as np
        N_NODES = 12500
        N_EDGES = 400000
        IN_FEATS = 256
        OUT_FEATS = 256
        dst, src = (edge_index[0], edge_index[1])
        agg = jnp.zeros_like(x).at[dst].set(x[src])
        h = jnp.concatenate((x, agg), axis=-1)
        return h @ W.T + b

    def _L0_ffn_ref(input_embeddings, router_w, w1, b1, w2, b2):
        import jax, jax.numpy as jnp
        import numpy as np
        NUM_EXPERTS = 8
        TOP_K = 2
        B, S, D = (8, 1024, 256)

        def _moe(tokens, router_w, w1, b1, w2, b2):
            N = tokens.shape[0]
            E = router_w.shape[0]
            logits = tokens.astype(jnp.float32) @ router_w.astype(jnp.float32).T
            probs = jax.nn.softmax(logits, axis=-1)
            rw, re = jax.lax.top_k(probs, TOP_K)
            if TOP_K > 1:
                rw = rw / jnp.maximum(rw.sum(-1, keepdims=True), 1e-12)
            rw = rw.astype(tokens.dtype)
            combine = jnp.zeros((N, E), tokens.dtype).at[jnp.arange(N)[:, None], re].set(rw)
            out = tokens
            for e in range(E):
                h = jax.nn.gelu(tokens @ w1[e] + b1[e], approximate=False)
                y = h @ w2[e] + b2[e]
                out = out + combine[:, e:e + 1] * y
            return out
        b, s, d = input_embeddings.shape
        tokens = input_embeddings.reshape(b * s, d)
        return _moe(tokens, router_w, w1, b1, w2, b2).reshape(b, s, d)
    edge_index = jnp.stack([src, dst])
    x = x + _L0_gnn_ref(_layernorm(x, axis=-1), edge_index, L0_gnn_W, L0_gnn_b)
    x = x + _L0_ffn_ref(_layernorm(x, axis=-1)[None], L0_ffn_router_w, L0_ffn_w1, L0_ffn_b1, L0_ffn_w2, L0_ffn_b2)[0]
    return x

_drawn_inputs = setup_inputs


def setup_inputs(seed=0):
    import zlib

    import numpy as np

    out = dict(_drawn_inputs(seed))
    spreads = {'L0_ffn_b1': (0.0, 0.349), 'L0_ffn_b2': (0.0, 0.1)}
    factors = {}
    for name, (base, spread) in spreads.items():
        noise = np.random.default_rng([zlib.crc32(name.encode()), seed]).standard_normal(out[name].shape)
        drawn = base * np.exp(spread * noise) if base else spread * noise
        out[name] = jnp.asarray(drawn.astype(out[name].dtype))
    for name, factor in factors.items():
        out[name] = (out[name] * factor).astype(out[name].dtype)
    return out
```

```python
import concourse.bass as bass
from concourse import mybir
from concourse.alu_op_type import AluOpType as ALU
from contextlib import ExitStack

P = 128
N = 12500
D = 256
E = 8
EDGES = 200000
T = (N + P - 1) // P
TAIL = N - (T - 1) * P
NP = T * P
CH = 125
NCH = EDGES // CH
GC = 32
NG = NCH // GC
BITS = 7
EXP0 = 15
BK = 16
KEY = 16384
B = 7
NB = T // B
XT = 256
RB = 14
R = 1 << RB
assert R >= NP + XT
NT = (2 * NP + E * (XT - 1)) // XT + 1
DUMMY = NT - 2 * NP // XT
ROWS = E * R + DUMMY * XT
SCALE = 64.0
EPS = 1e-5


class Count:

    def __init__(self, eng, sem):
        self.eng, self.sem, self.base, self.n = eng, sem, 0, 0

    def start(self, base):
        self.base, self.n = base, 0

    def done(self, instruction):
        instruction.then_inc(self.sem, 1)
        self.n += 1

    def settle(self):
        self.eng.wait_ge(self.sem, self.base + self.n)


def gnn_moe(nc, x, src_cols, edge_rows, wg, bg, rw, w1, b1, w2, b2, out):
    f32, f16, bf16, i32, u8 = (mybir.dt.float32, mybir.dt.float16, mybir.dt.bfloat16, mybir.dt.int32,
                               mybir.dt.uint8)
    ACT = mybir.ActivationFunctionType
    AX = mybir.AxisListType
    ds = bass.ds
    SIZE = {f32: 4, i32: 4, f16: 2, bf16: 2}

    agg_rows = nc.dram_tensor("agg_rows", [NP + P, D], f32).ap()
    tok_rows = nc.dram_tensor("tok_rows", [ROWS, 2 * D], f16).ap()
    y_rows = nc.dram_tensor("y_rows", [NT * XT, D], f32).ap()

    ctx = ExitStack()
    with ctx:
        def sb(name, shape, dt):
            return ctx.enter_context(nc.sbuf_tensor(name, shape, dt))

        def sem(name):
            return ctx.enter_context(nc.semaphore(name))

        xs = sb("xs", [P, T, D], f32)
        w1s = sb("w1s", [P, 2, E, 2, D], f16)
        w2s = sb("w2s", [P, 2, E, 2, D], f16)
        wgs = sb("wgs", [P, 2, 2, 2 * D], f16)
        rws = sb("rws", [P, 2, E], f32)
        b1s = sb("b1s", [P, E, 2], f32)
        b2s = sb("b2s", [P, E, D], f32)
        bgs = sb("bgs", [P, D], f32)
        ident = sb("ident", [P, P], f32)
        identh = sb("identh", [P, P], f16)
        mv = sb("mv", [P, T, 2], f32)
        rstd = sb("rstd", [P, T], f32)
        nmr = sb("nmr", [P, T], f32)
        mvb = sb("mvb", [P, B, 2], f32)
        bst3 = sb("bst3", [P, B, 6], f32)
        base8 = sb("base8", [P, E], f32)
        rank4 = sb("rank4", [P, E], f32)[:, :]
        one8 = sb("one8", [P, 1], f32)
        zcol = sb("zcol", [P, 1], f32)
        eps = sb("eps", [P, 1], f32)
        cid = sb("cid", [P, T], i32)
        nid = sb("nid", [P, T], f32)
        gat = sb("gat", [P, T], i32)
        slots = sb("slots", [P, 2, T], i32)
        comb = sb("comb", [P, 2, T], f32)
        cnt = sb("cnt", [P, E], f32)
        tab = sb("tab", [P, 2, NT], i32)

        arena_bytes = 59680
        arena = sb("arena", [P, arena_bytes], u8)

        class Arena:
            def __init__(self):
                self.at = 0

            def take(self, shape, dt):
                n = SIZE[dt]
                for s in shape[1:]:
                    n *= s
                a = arena[0:shape[0], self.at:self.at + n].bitcast(dt)
                self.at += (n + 31) // 32 * 32
                assert self.at <= arena_bytes, self.at
                names = "abcd"[:len(shape) - 1]
                if len(names) > 1:
                    a = a.rearrange(f"p ({' '.join(names)}) -> p {' '.join(names)}",
                                    **{k: s for k, s in zip(names, shape[1:])})
                return a

        one = Arena()
        lohi = one.take([CH, 2 * NG, 2, BK], f32)
        oh_lo = one.take([CH, 2, BK, P], bf16)
        oh_hi = one.take([CH, 2, BK, T], bf16)
        vbuf = one.take([P, NG, T], i32)
        stage = one.take([CH, 2, 2 * BK], f32)
        iota = one.take([P, P], bf16)
        xn = one.take([P, 2, D], f32)
        xh = one.take([P, 2, D], f16)
        xl = one.take([P, 2, D], f16)
        pb = one.take([P, 2, D], f32)
        wst = one.take([P, 2, 2, D], f32)
        srcs = vbuf[0:CH, 0:17, :].rearrange("p a b -> p (a b)")[:, 0:NCH]
        part = vbuf[0:CH, 17:34, :].rearrange("p a b -> p (a b)")[:, 0:NCH]
        wgf = vbuf[:, 34:45, :].rearrange("p a b -> p (a b)")[:, 0:4 * D].bitcast(f32)
        fbuf = Arena().take([P, NG, T], f32)

        two = Arena()
        g256 = one.take([P, NG], f32)
        er = two.take([P, 2, B, 2 * CH], i32)
        two.at = max(two.at, 33000)
        kcode = two.take([P, CH], f32)
        ekey = two.take([P, B, CH], f32)
        eeq = two.take([P, B, CH], f32)
        wm = two.take([P, B], f32)
        wmi = two.take([P, B], i32)
        wabs = two.take([P, B], f32)
        cst = two.take([P, 2, B], i32)

        three = Arena()
        pg = three.take([P, 2, B, D], f32)
        thl = three.take([P, 2, B, 2 * D], f16)
        t32 = three.take([P, B, D], f32)
        tT = three.take([P, 2, D], f32)
        tri = three.take([P, P], bf16)
        ones = three.take([P, P], bf16)
        rank = three.take([P, E], f32)
        eoff = three.take([P, E], f32)
        lg = three.take([P, B, E], f32)
        lex = three.take([P, B, E], f32)
        pr = three.take([P, B, E], f32)
        tmp = three.take([P, B, E], f32)
        oh1 = three.take([P, B, E], f32)
        oh2 = three.take([P, B, E], f32)
        msk = three.take([P, B + 1, E], bf16)
        pos = three.take([P, B, E], f32)
        r7 = three.take([P, 8, B], f32)
        sidx = three.take([P, 2, 2, B], i32)
        pidx = three.take([P, 2, B], i32)
        zt = three.take([P, 2 * D], f16)
        zidx = three.take([P, E, 2], i32)
        zof = three.take([P, E, 2], f32)
        nt8 = three.take([P, E], i32)
        ntf = three.take([P, E], f32)
        cend = three.take([P, E], f32)
        zero8 = three.take([P, E], f32)

        four = Arena()
        xd = four.take([P, 2, 2, 2 * D], f16)
        xT = four.take([P, 2, 2, 2, XT], f16)
        h32 = four.take([P, 2, 2, XT], f32)
        hh = four.take([P, 2, 2, XT], f16)
        hl = four.take([P, 2, 2, XT], f16)
        yb = four.take([P, 2, 2, D], f32)
        jidx = four.take([P, NT], f32)
        tge = four.take([P, NT, E], f32)
        tgn = four.take([P, NT, E], f32)
        tej = four.take([P, NT], f32)
        tst = four.take([P, NT], f32)
        start = four.take([P, E], f32)
        which = four.take([P, 2 * T], i32)
        whichf = four.take([P, 2 * T], f32)
        chosen = four.take([P, 2 * T, E], f32)

        five = Arena()
        yg = five.take([P, 2, 2, B, D], f32)
        yidx = five.take([P, 2, 2, B], i32)

        bank = [ctx.enter_context(nc.psum_tensor(f"bank{i}", [P, 512], f32)) for i in range(8)]

        s_src, s_small, s_wg = sem("s_src"), sem("s_small"), sem("s_wg")
        s_x = [sem(f"s_x{i}") for i in range(NB // 2)]
        s_wst = [sem("s_wst0"), sem("s_wst1")]
        w_prep = sem("w_prep")
        zeroed, iota_ready, consts_ready = sem("zeroed"), sem("iota_ready"), sem("consts_ready")
        pool_done, vec_done = sem("pool_done"), sem("vec_done")
        passed, turn = sem("passed"), sem("turn")
        std_ready, ln_ready, var_ready = sem("std_ready"), sem("ln_ready"), sem("var_ready")
        onehots_ready, onehots_used, last_ready, last_taken = (sem("onehots_ready"), sem("onehots_used"),
                                                               sem("last_ready"), sem("last_taken"))
        xn_ready, xt_ready, xh_ready, xl_ready = sem("xn_ready"), sem("xt_ready"), sem("xh_ready"), sem("xl_ready")
        g_ready, self_added, agg_copied, agg_biased = (sem("g_ready"), sem("self_added"), sem("agg_copied"),
                                                       sem("agg_biased"))
        agg_stored = [sem("agg_stored0"), sem("agg_stored1")]
        s_brow = sem("s_brow")
        cid_ready = sem("cid_ready")
        er_full = [sem("er_full0"), sem("er_full1")]
        gat_ready = sem("gat_ready")
        consts3_ready = sem("consts3_ready")
        pidx_ready = sem("pidx_ready")
        pg_full = [sem("pg_full0"), sem("pg_full1")]
        pg_used = sem("pg_used")
        t_ready, tt_ready, ttc_ready, lg_ready = sem("t_ready"), sem("tt_ready"), sem("ttc_ready"), sem("lg_ready")
        tparts_ready = sem("tparts_ready")
        ldiff_ready, lexp_ready, msk_ready, pos_ready, sidx_ready = (sem("ldiff_ready"), sem("lexp_ready"),
                                                                     sem("msk_ready"), sem("pos_ready"),
                                                                     sem("sidx_ready"))
        scattered = [sem("scattered0"), sem("scattered1")]
        zidx_ready, zeros_stored, dummies_stored = sem("zidx_ready"), sem("zeros_stored"), sem("dummies_stored")
        all_stored, tab_ready, jidx_ready, zt_ready = sem("all_stored"), sem("tab_ready"), sem("jidx_ready"), sem("zt_ready")
        xd_full = [sem("xd_full0"), sem("xd_full1")]
        xt4_ready, xt4_hi, xt4_lo, h_ready, gelu_ready, hh_ready, hl_ready, y_ready, y_taken = (
            sem(n) for n in ("xt4_ready", "xt4_hi", "xt4_lo", "h_ready", "gelu_ready", "hh_ready", "hl_ready",
                             "y_ready", "y_taken"))
        y_stored = [sem("y_stored0"), sem("y_stored1")]
        experts_done, yidx_ready = sem("experts_done"), sem("yidx_ready")
        yg_full = [sem("yg_full0"), sem("yg_full1")]
        out_ready, s_out = sem("out_ready"), sem("s_out")

        block = ctx.enter_context(nc.Block())
        x_chunk = T // len(s_x)

        def tokens(a, t, n):
            return a[ds(t * P, n * P), :].rearrange("(s p) d -> p s d", p=P)

        @block.sync
        def _(sp):
            sp.dma_start(srcs, src_cols).then_inc(s_src, 16)
            sp.dma_start(bgs[:, :], bg.rearrange("(a d) -> a d", a=1).broadcast_to([P, D])).then_inc(s_small, 16)
            sp.dma_start(wgf, wg).then_inc(s_wg, 16)
            for c in range(len(s_x)):
                n = x_chunk if c < len(s_x) - 1 else x_chunk - 1
                sp.dma_start(xs[:, c * x_chunk:c * x_chunk + n, :], tokens(x, c * x_chunk, n)).then_inc(s_x[c], 16)
            sp.wait_ge(zeroed, 1)
            sp.dma_start(xs[0:TAIL, T - 1, :], x[(T - 1) * P:N, :]).then_inc(s_x[-1], 16)
            sp.dma_start(rws[:, :, :].rearrange("p a e -> p (a e)"), rw).then_inc(s_small, 16)
            sp.dma_start(b1s[:, :, :].rearrange("p a e -> p (a e)"), b1).then_inc(s_small, 16)
            sp.dma_start(b2s[:, :, :].rearrange("p a e -> p (a e)"),
                         b2.rearrange("e d -> (e d)").rearrange("(a n) -> a n", a=1).broadcast_to([P, E * D])
                         ).then_inc(s_small, 16)
            sp.wait_ge(s_small, 64)
            sp.dma_start(agg_rows[NP:NP + P, :], bgs[:, :]).then_inc(s_brow, 16)

            def load_weight(w, e, u, k):
                if u >= 2:
                    sp.wait_ge(w_prep, u - 1)
                sp.dma_start(wst[:, k, :, :], w[e, :, :].rearrange("(c k) f -> k c f", k=P)).then_inc(s_wst[k], 16)

            def store_agg(i):
                for k in range(2):
                    sp.wait_ge(agg_biased, 2 * i + k + 1)
                    sp.dma_start(agg_rows[ds((2 * i + k) * P, P), :], pb[:, k, :]).then_inc(agg_stored[k], 16)

            for u in range(2 * E):
                load_weight(w1 if u < E else w2, u % E, u, u % 2)
                store_agg(u)
            with sp.Fori(2 * E, T // 2) as i:
                store_agg(i)

            sp.wait_ge(tab_ready, 1)
            sp.wait_ge(all_stored, 1)

            def load_tile(j, k, row):
                sp.dma_start(xd[:, k, :, :],
                             tok_rows[ds(row, XT), :].rearrange("(h p) d -> p h d", p=P)).then_inc(xd_full[k], 16)

            def store_tile(j, k):
                sp.wait_ge(y_taken, j + 1)
                sp.dma_start(y_rows[ds(j * XT, XT), :].rearrange("(h p) d -> p h d", p=P),
                             yb[:, k, :, :]).then_inc(y_stored[k], 16)

            def row_of(j):
                return sp.value_load(tab[0:1, 1, ds(j, 1)], min_val=0, max_val=ROWS - XT)

            for k in range(2):
                load_tile(k, k, row_of(k))
            with sp.Fori(0, NT // 2 - 1) as i:
                for k in range(2):
                    sp.wait_ge(xt4_ready, 2 * i + k + 1)
                    load_tile(2 * i + k + 2, k, row_of(2 * i + k + 2))
                    store_tile(2 * i + k, k)
            for k in range(2):
                store_tile(NT - 2 + k, k)
            for k in range(2):
                sp.wait_ge(y_stored[k], 16 * (NT // 2))
            sp.sem_inc(experts_done, 1)

            with sp.Fori(0, NB - 1) as b:
                sp.wait_ge(out_ready, b + 1)
                sp.dma_start(tokens(out, b * B, B), xs[:, ds(b * B, B), :]).then_inc(s_out, 16)
            sp.wait_ge(out_ready, NB)
            sp.dma_start(tokens(out, (NB - 1) * B, B - 1), xs[:, (NB - 1) * B:T - 1, :]).then_inc(s_out, 16)
            sp.dma_start(out[(T - 1) * P:N, :], xs[0:TAIL, T - 1, :]).then_inc(s_out, 16)
            sp.wait_ge(s_out, 16 * (NB + 1))

        @block.gpsimd
        def _(pool):
            did = Count(pool, pool_done)
            gp = nc.gpsimd
            gp.iota(iota, [[1, P]], 0, 0, allow_small_or_imprecise_dtypes=True).then_inc(iota_ready, 1)
            gp.memset(xs[:, T - 1, :], 0.0).then_inc(zeroed, 1)
            gp.memset(one8[:, :], 1.0).then_inc(consts_ready, 1)
            gp.memset(zcol[:, :], 0.0).then_inc(consts_ready, 1)
            gp.memset(eps[:, :], EPS).then_inc(iota_ready, 1)
            gp.iota(g256, [[256, NG]], 0, 0, allow_small_or_imprecise_dtypes=True).then_inc(consts_ready, 1)
            gp.iota(nid[:, :], [[P, T]], 0, 1, allow_small_or_imprecise_dtypes=True).then_inc(consts_ready, 1)
            did.done(gp.memset(ident[:, :], 0.0))
            did.done(gp.memset(identh[:, :], 0.0))
            did.settle()
            for m in (ident, identh):
                gp.affine_select(out=m[:, :], in_=m[:, :], compare_op=ALU.not_equal, fill=1.0, base=0,
                                 pattern=[[-1, P]], channel_multiplier=1).then_inc(consts_ready, 1)

            def prepare_weight(ws, e, u, k):
                pool.wait_ge(s_wst[k], 16 * (u // 2 + 1))
                did.done(gp.tensor_scalar(wst[:, k, :, :], wst[:, k, :, :], SCALE, None, ALU.mult))
                did.settle()
                did.done(gp.tensor_copy(ws[:, 0, e, :, :], wst[:, k, :, :]))
                did.settle()
                gp.tensor_tensor(ws[:, 1, e, :, :], wst[:, k, :, :], ws[:, 0, e, :, :],
                                 ALU.subtract).then_inc(w_prep, 1)

            def add_bias(i):
                for k in range(2):
                    pool.wait_ge(agg_copied, 2 * i + k + 1)
                    gp.tensor_tensor(pb[:, k, :], pb[:, k, :], bgs[:, :], ALU.add).then_inc(agg_biased, 1)

            pool.wait_ge(s_small, 64)
            for u in range(2 * E):
                prepare_weight(w1s if u < E else w2s, u % E, u, u % 2)
                add_bias(u)
            with pool.Fori(2 * E, T // 2) as i:
                add_bias(i)

            pool.wait_ge(cid_ready, 1)
            gp.iota(kcode, [[KEY, CH]], KEY, 0, allow_small_or_imprecise_dtypes=True).then_inc(consts_ready, 1)

            def gather_edges(b, k):
                pool.wait_ge(cid_ready, b + 2)
                pool.sem_inc(turn, 1)
                for s in range(B):
                    gp.indirect_dma_start(er[:, k, s, :], None, edge_rows,
                                          bass.IndirectOffsetOnAxis(cst[:, k, s:s + 1], 0)).then_inc(er_full[k], 16)

            with pool.Fori(0, NB // 2) as i:
                for k in range(2):
                    gather_edges(2 * i + k, k)

            pool.wait_ge(gat_ready, 1)
            did.done(gp.memset(tri, 1.0))
            did.done(gp.memset(ones, 1.0))
            did.done(gp.memset(msk, 0.0))
            did.done(gp.memset(zero8, 0.0))
            did.done(gp.iota(rank, [[-1, E]], E, 0, allow_small_or_imprecise_dtypes=True))
            did.done(gp.iota(eoff, [[1, E]], 0, 0, allow_small_or_imprecise_dtypes=True))
            did.done(gp.iota(zof, [[0, E], [P, 2]], 0, 1, allow_small_or_imprecise_dtypes=True))
            did.done(gp.memset(zt, 0.0))
            did.settle()
            gp.tensor_scalar(eoff, eoff, float(R), None, ALU.mult).then_inc(consts3_ready, 1)
            gp.affine_select(out=tri, in_=tri, compare_op=ALU.is_gt, fill=0.0, base=0,
                             pattern=[[1, P]], channel_multiplier=-1).then_inc(consts3_ready, 1)
            for j in range(2 * DUMMY):
                pool.dma_start(tok_rows[E * R + j * P:E * R + (j + 1) * P, :], zt).then_inc(dummies_stored, 16)
            for k in range(2):
                pool.wait_ge(agg_stored[k], 16 * (T // 2))
            pool.wait_ge(s_brow, 16)

            def gather_agg(b, k):
                pool.wait_ge(pidx_ready, b + 1)
                pool.sem_inc(turn, 1)
                for s in range(B):
                    gp.indirect_dma_start(pg[:, k, s, :], None, agg_rows,
                                          bass.IndirectOffsetOnAxis(pidx[:, k, s:s + 1], 0)).then_inc(pg_full[k], 16)

            def scatter_tokens(b, k):
                pool.wait_ge(sidx_ready, b + 1)
                pool.sem_inc(turn, 1)
                for s in range(B):
                    for r in range(2):
                        gp.indirect_dma_start(tok_rows, bass.IndirectOffsetOnAxis(sidx[:, k, r, s:s + 1], 0),
                                              thl[:, k, s, :], None).then_inc(scattered[k], 16)

            gather_agg(0, 0)
            with pool.Fori(0, NB // 2 - 1) as i:
                gather_agg(2 * i + 1, 1)
                scatter_tokens(2 * i, 0)
                gather_agg(2 * i + 2, 0)
                scatter_tokens(2 * i + 1, 1)
            gather_agg(NB - 1, 1)
            scatter_tokens(NB - 2, 0)
            scatter_tokens(NB - 1, 1)
            pool.wait_ge(zidx_ready, 1)
            for e in range(E):
                for h in range(2):
                    gp.indirect_dma_start(tok_rows, bass.IndirectOffsetOnAxis(zidx[:, e, h:h + 1], 0),
                                          zt, None).then_inc(zeros_stored, 16)
            for k in range(2):
                pool.wait_ge(scattered[k], 16 * 2 * B * (NB // 2))
            pool.wait_ge(zeros_stored, 16 * 2 * E)
            pool.wait_ge(dummies_stored, 16 * 2 * DUMMY)
            pool.sem_inc(all_stored, 1)
            pool.wait_ge(tab_ready, 1)

            pool.wait_ge(experts_done, 1)

            def gather_results(b, k):
                pool.wait_ge(yidx_ready, b + 1)
                pool.sem_inc(turn, 1)
                for s in range(B):
                    for r in range(2):
                        gp.indirect_dma_start(yg[:, k, r, s, :], None, y_rows,
                                              bass.IndirectOffsetOnAxis(yidx[:, k, r, s:s + 1], 0)
                                              ).then_inc(yg_full[k], 16)

            with pool.Fori(0, NB // 2) as i:
                for k in range(2):
                    gather_results(2 * i + k, k)

        @block.scalar
        def _(act):
            sc = nc.scalar
            act.wait_ge(var_ready, 1)
            act.wait_ge(iota_ready, 2)
            sc.activation(rstd[:, :], mv[:, :, 1], ACT.Sqrt, bias=eps[:, :]).then_inc(std_ready, 1)
            act.wait_ge(ln_ready, 1)

            def node_pair(i, first):
                for k in range(2):
                    t = 2 * i + k
                    sc.activation(xn[:, k, :], xs[:, ds(t, 1), :].rearrange("p a d -> p (a d)"), ACT.Identity,
                                  bias=nmr[:, ds(t, 1)], scale=rstd[:, ds(t, 1)]).then_inc(xn_ready, 1)
                for k in range(2):
                    act.wait_ge(xt_ready, 2 * i + k + 1)
                    sc.activation(xh[:, k, :], bank[k][:, 0:D], ACT.Copy).then_inc(xh_ready, 1)
                for k in range(2):
                    act.wait_ge(g_ready, 2 * i + k + 1)
                    if not first:
                        act.wait_ge(agg_stored[k], 16 * i)
                    sc.activation(pb[:, k, :], bank[5 + k][:, 0:D], ACT.Copy,
                                  scale=1.0 / SCALE).then_inc(agg_copied, 1)

            node_pair(0, True)
            with act.Fori(1, T // 2) as i:
                node_pair(i, False)

            def token_batch(b, k):
                act.wait_ge(var_ready, b + 2)
                sc.activation(rstd[:, ds(b * B, B)], mv[:, ds(b * B, B), 1], ACT.Sqrt,
                              bias=eps[:, :]).then_inc(std_ready, 1)
                act.wait_ge(ln_ready, b + 2)
                for s in range(B):
                    t = b * B + s
                    sc.activation(t32[:, s, :], xs[:, ds(t, 1), :].rearrange("p a d -> p (a d)"), ACT.Identity,
                                  bias=nmr[:, ds(t, 1)], scale=rstd[:, ds(t, 1)]).then_inc(t_ready, 1)
                for s in range(B):
                    act.wait_ge(tt_ready, b * B + s + 1)
                    sc.activation(tT[:, s % 2, :], bank[s % 2][:, 0:D], ACT.Copy).then_inc(ttc_ready, 1)
                act.wait_ge(ldiff_ready, b + 1)
                sc.activation(lex, lg, ACT.Exp).then_inc(lexp_ready, 1)

            with act.Fori(0, NB // 2) as i:
                for k in range(2):
                    token_batch(2 * i + k, k)

            act.wait_ge(tab_ready, 1)

            def expert_tile(j, k, e, first):
                act.wait_ge(xt4_ready, j + 1)
                if not first:
                    act.wait_ge(h_ready, j - 1)
                sc.activation(xT[:, k, 0, :, :].rearrange("p a b -> p (a b)"),
                              bank[k][:, :].bitcast(f16)[:, 0:2 * XT], ACT.Copy).then_inc(xt4_hi, 1)
                act.wait_ge(h_ready, j + 1)
                if not first:
                    act.wait_ge(hl_ready, j - 1)
                for c in range(2):
                    last = sc.activation(h32[:, k, c, :], bank[2 + k][:, c * XT:(c + 1) * XT], ACT.Gelu,
                                         bias=b1s[:, ds(e, 1), c], scale=1.0 / SCALE)
                last.then_inc(gelu_ready, 1)

            def pair_of_tiles(i, first):
                for k in range(2):
                    e = act.value_load(tab[0:1, 0, ds(2 * i + k, 1)], min_val=0, max_val=E - 1)
                    expert_tile(2 * i + k, k, e, first)

            pair_of_tiles(0, True)
            with act.Fori(1, NT // 2) as i:
                pair_of_tiles(i, False)

        @block.tensor
        def _(pe):
            mm = nc.tensor.matmul
            pe.wait_ge(consts_ready, 6)

            def block_of_chunks(i, s, first):
                pe.wait_ge(onehots_ready, 2 * i + s + 1)
                if s == 0 and not first:
                    pe.wait_ge(last_taken, i)
                for c in range(BK):
                    last = mm(bank[4][:, 0:T], oh_lo[:, s, c, :], oh_hi[:, s, c, :],
                              start=(s == 0 and c == 0), stop=(s == 1 and c == BK - 1))
                last.then_inc(onehots_used, 1)

            def node_linear(i, k, first):
                pe.wait_ge(xh_ready, 2 * i + k + 1)
                pe.wait_ge(xl_ready, 2 * i + k + 1)
                if not first:
                    pe.wait_ge(self_added, 2 * i + k - 1)
                    pe.wait_ge(agg_copied, 2 * i + k - 1)
                n = 0
                for c in range(2):
                    for a, w in ((xh, 0), (xh, 1), (xl, 0)):
                        for to, half in ((bank[2 + k], 0), (bank[5 + k], 1)):
                            last = mm(to[:, 0:D], a[:, k, c * P:(c + 1) * P], wgs[:, w, c, half * D:(half + 1) * D],
                                      start=(n == 0), stop=(n == 5))
                        n += 1
                last.then_inc(g_ready, 1)

            def node_pair(i, first):
                for k in range(2):
                    pe.wait_ge(xn_ready, 2 * i + k + 1)
                    if not first:
                        pe.wait_ge(xl_ready, 2 * i + k - 1)
                    for c in range(2):
                        last = nc.tensor.transpose(bank[k][:, c * P:(c + 1) * P], xn[:, k, c * P:(c + 1) * P],
                                                   ident[:, :])
                    last.then_inc(xt_ready, 1)
                block_of_chunks(i, 0, first)
                node_linear(i, 0, first)
                node_linear(i, 1, first)
                block_of_chunks(i, 1, first)

            node_pair(0, True)
            with pe.Fori(1, T // 2) as i:
                node_pair(i, False)
            block_of_chunks(NG - 1, 0, False)
            block_of_chunks(NG - 1, 1, False)

            pe.wait_ge(consts3_ready, 2)

            def token_batch(b, k, first):
                for s in range(B + 1):
                    if s < B:
                        pe.wait_ge(t_ready, b * B + s + 1)
                        if not (first and s < 2):
                            pe.wait_ge(ttc_ready, b * B + s - 1)
                        for c in range(2):
                            last = nc.tensor.transpose(bank[s % 2][:, c * P:(c + 1) * P],
                                                       t32[:, s, c * P:(c + 1) * P], ident[:, :])
                        last.then_inc(tt_ready, 1)
                    if s >= 1:
                        q = s - 1
                        pe.wait_ge(ttc_ready, b * B + q + 1)
                        for c in range(2):
                            last = mm(bank[2][:, q * E:(q + 1) * E], tT[:, q % 2, c * P:(c + 1) * P], rws[:, c, :],
                                      start=(c == 0), stop=(c == 1))
                last.then_inc(lg_ready, 1)
                pe.wait_ge(msk_ready, b + 1)
                places = bank[3][:, 0:(B + 1) * E]
                mm(places, tri, msk.rearrange("p a e -> p (a e)"), start=True, stop=False)
                for s in range(B):
                    n = B - s
                    last = mm(bank[3][:, (s + 1) * E:(B + 1) * E].rearrange("p (a e) -> p a e", e=E), ones,
                              msk[:, s:s + 1, :].broadcast_to([P, n, E]), start=False, stop=(s == B - 1))
                last.then_inc(pos_ready, 1)

            token_batch(0, 0, True)
            token_batch(1, 1, False)
            with pe.Fori(1, NB // 2) as i:
                for k in range(2):
                    token_batch(2 * i + k, k, False)

            pe.wait_ge(tab_ready, 1)
            pe.wait_ge(w_prep, 2 * E)

            def tile_in(i, k, first):
                j = 2 * i + k
                pe.wait_ge(xd_full[k], 16 * i + 16)
                if not first:
                    pe.wait_ge(xt4_hi, j - 1)
                    pe.wait_ge(xt4_lo, j - 1)
                for w in range(2):
                    flip = bank[k + 6 * w][:, :].bitcast(f16)
                    for c in range(2):
                        for h in range(2):
                            at = c * XT + h * P
                            last = nc.tensor.transpose(flip[:, at:at + P],
                                                       xd[:, k, h, w * D + c * P:w * D + (c + 1) * P], identh[:, :])
                last.then_inc(xt4_ready, 1)

            def tile_hidden(i, k, e, first):
                j = 2 * i + k
                pe.wait_ge(xt4_hi, j + 1)
                pe.wait_ge(xt4_lo, j + 1)
                if not first:
                    pe.wait_ge(gelu_ready, j - 1)
                for f in range(2):
                    n = 0
                    for c in range(2):
                        for w, a in ((0, 0), (0, 1), (1, 0)):
                            last = mm(bank[2 + k][:, f * XT:(f + 1) * XT],
                                      w1s[:, w, ds(e, 1), c, f * P:(f + 1) * P].rearrange("p a f -> p (a f)"),
                                      xT[:, k, a, c, :], start=(n == 0), stop=(n == 5))
                            n += 1
                last.then_inc(h_ready, 1)

            def tile_out(i, k, e, first):
                j = 2 * i + k
                pe.wait_ge(hh_ready, j + 1)
                pe.wait_ge(hl_ready, j + 1)
                if not first:
                    pe.wait_ge(y_taken, j - 1)
                for h in range(2):
                    n = 0
                    for c in range(2):
                        for a, w in ((hh, 0), (hh, 1), (hl, 0)):
                            last = mm(bank[4 + k][:, h * D:(h + 1) * D], a[:, k, c, h * P:(h + 1) * P],
                                      w2s[:, w, ds(e, 1), c, :].rearrange("p a d -> p (a d)"),
                                      start=(n == 0), stop=(n == 5))
                            n += 1
                last.then_inc(y_ready, 1)

            def pair_of_tiles(i, first):
                e = [pe.value_load(tab[0:1, 0, ds(2 * i + k, 1)], min_val=0, max_val=E - 1) for k in range(2)]
                tile_in(i, 0, first)
                tile_in(i, 1, first)
                tile_hidden(i, 0, e[0], first)
                tile_hidden(i, 1, e[1], first)
                tile_out(i, 0, e[0], first)
                tile_out(i, 1, e[1], first)

            pair_of_tiles(0, True)
            with pe.Fori(1, NT // 2) as i:
                pair_of_tiles(i, False)

        @block.vector
        def _(dve):
            ve = nc.vector
            did = Count(dve, vec_done)

            dve.wait_ge(s_src, 16)
            for half, (op, by) in enumerate(((ALU.bitwise_and, P - 1), (ALU.logical_shift_right, 7))):
                did.done(ve.tensor_scalar(part, srcs, by, None, op))
                did.settle()
                did.done(ve.tensor_copy(lohi[:, :, half, :], part.rearrange("p (g c) -> p g c", c=BK)))
                did.settle()
            dve.wait_ge(s_wg, 16)
            did.done(ve.tensor_scalar(wgf, wgf, SCALE, None, ALU.mult))
            did.settle()
            did.done(ve.tensor_copy(wgs[:, 0, :, :].rearrange("p a b -> p (a b)"), wgf))
            did.settle()
            did.done(ve.tensor_tensor(wgs[:, 1, :, :].rearrange("p a b -> p (a b)"), wgf,
                                      wgs[:, 0, :, :].rearrange("p a b -> p (a b)"), ALU.subtract))
            first_stats = did.n
            def layer_statistics(b):
                for s in range(B):
                    did.done(ve.bn_stats(bst3[:, s, :], xs[:, ds(b * B + s, 1), :].rearrange("p a d -> p (a d)")))
                did.settle()
                dve.sem_inc(passed, 1)
                for s in range(B):
                    did.done(ve.bn_aggr(mvb[:, s, :], bst3[:, s, :]))
                did.settle()
                did.done(ve.tensor_copy(mv[:, ds(b * B, B), :], mvb[:, :, :]))

            per = 2 * B + 1
            for c in range(len(s_x)):
                dve.wait_ge(s_x[c], 16 if c < len(s_x) - 1 else 32)
                for k in range(2):
                    did.start(first_stats + (2 * c + k) * per)
                    layer_statistics(2 * c + k)
            did.settle()
            dve.sem_inc(var_ready, 1)
            dve.wait_ge(std_ready, 1)
            did.done(ve.reciprocal(rstd[:, :], rstd[:, :]))
            did.settle()
            ve.scalar_tensor_tensor(nmr[:, :], mv[:, :, 0], -1.0, rstd[:, :], ALU.mult, ALU.mult).then_inc(ln_ready, 1)
            before = did.base + did.n

            dve.wait_ge(iota_ready, 2)
            dve.wait_ge(consts_ready, 6)

            def block_of_onehots(i, s, first):
                if not first:
                    dve.wait_ge(onehots_used, 2 * i + s - 1)
                for c in range(BK):
                    ve.tensor_scalar(oh_lo[:, s, c, :], iota[0:CH, :], stage[:, s, c:c + 1], None,
                                     ALU.is_equal)
                    j = s * BK + c
                    last = ve.tensor_scalar(oh_hi[:, s, c, :], iota[0:CH, 0:T], stage[:, s, BK + c:BK + c + 1],
                                            2.0 ** (BITS * j + EXP0 - 127), ALU.is_equal, ALU.mult)
                last.then_inc(onehots_ready, 1)

            def take_group(g):
                dve.wait_ge(onehots_used, 2 * g + 2)
                ve.tensor_scalar(vbuf[:, ds(g, 1), :].rearrange("p a t -> p (a t)"), bank[4][:, 0:T].bitcast(i32), 23,
                                 None, ALU.logical_shift_right).then_inc(last_taken, 1)

            def take_stage(i, s, first):
                if not first:
                    dve.wait_ge(onehots_ready, 2 * i + s - 1)
                did.done(ve.tensor_copy(stage[:, s, :],
                                        lohi[:, ds(2 * i + s, 1), :, :].rearrange("p g a c -> p (g a c)")))

            def node_pair(i, first):
                did.start(before + 1 + 2 * i)
                did.settle()
                take_stage(i, 1, first)
                block_of_onehots(i, 0, first)
                if not first:
                    take_group(i - 1)
                for k in range(2):
                    dve.wait_ge(xh_ready, 2 * i + k + 1)
                    ve.tensor_tensor(xl[:, k, :], bank[k][:, 0:D], xh[:, k, :], ALU.subtract).then_inc(xl_ready, 1)
                did.settle()
                take_stage(i + 1, 0, False)
                block_of_onehots(i, 1, first)
                for k in range(2):
                    dve.wait_ge(g_ready, 2 * i + k + 1)
                    xt_ = xs[:, ds(2 * i + k, 1), :].rearrange("p a d -> p (a d)")
                    ve.scalar_tensor_tensor(xt_, bank[2 + k][:, 0:D], 1.0 / SCALE, xt_, ALU.mult,
                                            ALU.add).then_inc(self_added, 1)

            did.start(before)
            take_stage(0, 0, True)
            node_pair(0, True)
            with dve.Fori(1, T // 2) as i:
                node_pair(i, False)
            did.start(before + 1 + T)
            did.settle()
            take_stage(NG - 1, 1, False)
            block_of_onehots(NG - 1, 0, False)
            take_group(NG - 2)
            did.settle()
            block_of_onehots(NG - 1, 1, False)
            take_group(NG - 1)
            dve.wait_ge(last_taken, NG)

            def step(instruction):
                did.done(instruction)
                did.settle()

            step(ve.scalar_tensor_tensor(fbuf, vbuf, 0.0, g256[:, :].unsqueeze(2).broadcast_to([P, NG, T]), ALU.is_gt,
                                         ALU.mult))
            step(ve.tensor_tensor(fbuf, fbuf, vbuf, ALU.add))
            step(ve.tensor_reduce(rstd[:, :], fbuf.rearrange("p g t -> p t g"), AX.X, ALU.max))
            group, field = gat, slots[:, 0, :]
            step(ve.tensor_copy(cid[:, :], rstd[:, :]))
            step(ve.tensor_scalar(group[:, :], cid[:, :], 8, None, ALU.logical_shift_right))
            step(ve.tensor_scalar(field, cid[:, :], 255, None, ALU.bitwise_and))
            step(ve.tensor_scalar(nmr[:, :], field, float(EXP0), 0.0, ALU.subtract, ALU.max))
            step(ve.tensor_scalar(field, nmr[:, :], 293.0, None, ALU.mult))
            step(ve.tensor_scalar(field, field, 11, None, ALU.logical_shift_right))
            step(ve.scalar_tensor_tensor(cid[:, :], group[:, :], float(GC), field, ALU.mult, ALU.add))
            dve.sem_inc(cid_ready, 1)
            before2 = did.base + did.n
            PER2 = 9

            def give_chunks(b, k):
                ve.tensor_copy(cst[:, k, :], cid[:, ds(b * B, B)]).then_inc(cid_ready, 1)

            def edge_batch(b, k, i, ahead):
                dve.wait_ge(er_full[k], 16 * B * i + 16 * B)
                did.done(ve.tensor_tensor(ekey, er[:, k, :, CH:2 * CH],
                                          kcode.unsqueeze(1).broadcast_to([P, B, CH]), ALU.add))
                did.done(ve.tensor_tensor(eeq, er[:, k, :, 0:CH],
                                          nid[:, ds(b * B, B)].unsqueeze(2).broadcast_to([P, B, CH]), ALU.is_equal))
                did.settle()
                if ahead:
                    give_chunks(b + 2, k)
                step(ve.tensor_tensor(eeq, eeq, ekey, ALU.mult))
                step(ve.tensor_reduce(wm, eeq, AX.X, ALU.max))
                did.done(ve.tensor_copy(wmi, wm))
                did.done(ve.tensor_scalar(wabs, wm, 0.0, float(NP), ALU.is_equal, ALU.mult))
                did.settle()
                step(ve.tensor_scalar(wmi, wmi, KEY - 1, None, ALU.bitwise_and))
                step(ve.tensor_tensor(gat[:, ds(b * B, B)], wmi, wabs, ALU.add))

            dve.wait_ge(consts_ready, 7)
            did.start(before2)
            give_chunks(0, 0)
            give_chunks(1, 1)
            with dve.Fori(0, NB // 2 - 1) as i:
                for k in range(2):
                    did.start(before2 + (2 * i + k) * (PER2 - 1))
                    edge_batch(2 * i + k, k, i, True)
            for k in range(2):
                did.start(before2 + (NB - 2 + k) * (PER2 - 1))
                edge_batch(NB - 2 + k, k, NB // 2 - 1, False)
            assert did.n == PER2 - 1
            before3 = did.base + did.n
            dve.sem_inc(gat_ready, 1)
            dve.wait_ge(consts3_ready, 2)

            def give_rows(b, k):
                did.done(ve.tensor_copy(pidx[:, k, :], gat[:, ds(b * B, B)]))
                did.settle()
                dve.sem_inc(pidx_ready, 1)

            def token_batch(b, k, i, first, ahead):
                def bc(a):
                    return a.unsqueeze(2).broadcast_to([P, B, E])

                if ahead:
                    give_rows(b + 1, 1 - k)
                else:
                    did.n += 1
                dve.wait_ge(pg_full[k], 16 * B * i + 16 * B)
                xb = xs[:, ds(b * B, B), :]
                step(ve.tensor_tensor(xb, xb, pg[:, k, :, :], ALU.add))
                dve.sem_inc(passed, 1)
                layer_statistics(b)
                did.settle()
                dve.sem_inc(var_ready, 1)
                dve.wait_ge(std_ready, b + 2)
                rb, nb = rstd[:, ds(b * B, B)], nmr[:, ds(b * B, B)]
                step(ve.reciprocal(rb, rb))
                ve.scalar_tensor_tensor(nb, mv[:, ds(b * B, B), 0], -1.0, rb, ALU.mult, ALU.mult).then_inc(ln_ready, 1)
                dve.wait_ge(t_ready, b * B + B)
                if not first:
                    dve.wait_ge(scattered[k], 16 * 2 * B * i)
                hi, lo = thl[:, k, :, 0:D], thl[:, k, :, D:2 * D]
                step(ve.tensor_copy(hi, t32))
                step(ve.tensor_tensor(lo, t32, hi, ALU.subtract))
                step(ve.tensor_tensor(xb, xb, t32, ALU.add))
                dve.wait_ge(lg_ready, b + 1)
                m, q, d, c1, c2 = (r7[:, n, :] for n in range(5))
                logit = bank[2][:, 0:B * E].rearrange("p (a e) -> p a e", e=E)
                step(ve.tensor_reduce(m, logit, AX.X, ALU.max))
                did.done(ve.tensor_tensor(lg, logit, bc(m), ALU.subtract))
                did.settle()
                dve.sem_inc(ldiff_ready, 1)
                dve.wait_ge(lexp_ready, b + 1)
                step(ve.tensor_reduce(q, lex, AX.X, ALU.add))
                step(ve.reciprocal(q, q))
                step(ve.tensor_tensor(pr, lex, bc(q), ALU.mult))
                rk = rank.unsqueeze(1).broadcast_to([P, B, E])

                def pick(top, hot):
                    step(ve.tensor_reduce(top, pr, AX.X, ALU.max))
                    step(ve.tensor_tensor(tmp, pr, bc(top), ALU.is_equal))
                    step(ve.tensor_tensor(tmp, tmp, rk, ALU.mult))
                    step(ve.tensor_reduce(q, tmp, AX.X, ALU.max))
                    step(ve.tensor_tensor(hot, rk, bc(q), ALU.is_equal))

                pick(c1, oh1)
                step(ve.scalar_tensor_tensor(pr, oh1, -2.0, pr, ALU.mult, ALU.add))
                pick(c2, oh2)
                step(ve.tensor_tensor(d, c1, c2, ALU.add))
                step(ve.tensor_scalar(d, d, 1e-12, None, ALU.max))
                step(ve.reciprocal(d, d))
                did.done(ve.tensor_tensor(comb[:, 0, ds(b * B, B)], c1, d, ALU.mult))
                did.done(ve.tensor_tensor(comb[:, 1, ds(b * B, B)], c2, d, ALU.mult))
                did.done(ve.tensor_tensor(msk[:, 0:B, :], oh1, oh2, ALU.add))
                did.settle()
                dve.sem_inc(msk_ready, 1)
                dve.wait_ge(pos_ready, b + 1)
                place = bank[3][:, 0:B * E].rearrange("p (a e) -> p a e", e=E)
                step(ve.tensor_tensor(pos, place, base8[:, :].unsqueeze(1).broadcast_to([P, B, E]), ALU.add))
                for r, hot in ((0, oh1), (1, oh2)):
                    step(ve.tensor_tensor(tmp, hot, pos, ALU.mult))
                    step(ve.tensor_reduce(c1 if r == 0 else c2, tmp, AX.X, ALU.add))
                for r, v in ((0, c1), (1, c2)):
                    did.done(ve.tensor_copy(sidx[:, k, r, :], v))
                    did.done(ve.tensor_copy(slots[:, r, ds(b * B, B)], v))
                did.done(ve.tensor_tensor(base8[:, :], base8[:, :], bank[3][:, B * E:(B + 1) * E], ALU.add))
                did.settle()
                dve.sem_inc(sidx_ready, 1)

            step(ve.tensor_copy(base8[:, :], eoff))
            give_rows(0, 0)
            start3 = before3 + 2
            did.start(start3)
            token_batch(0, 0, 0, True, True)
            PER3 = did.n
            did.start(start3 + PER3)
            token_batch(1, 1, 0, True, True)
            with dve.Fori(1, NB // 2 - 1) as i:
                for k in range(2):
                    did.start(start3 + (2 * i + k) * PER3)
                    token_batch(2 * i + k, k, i, False, True)
            did.start(start3 + (NB - 2) * PER3)
            token_batch(NB - 2, 0, NB // 2 - 1, False, True)
            did.start(start3 + (NB - 1) * PER3 - 1)
            token_batch(NB - 1, 1, NB // 2 - 1, False, False)

            step(ve.tensor_tensor(zof, zof, base8[:, :].unsqueeze(2).broadcast_to([P, E, 2]), ALU.add))
            step(ve.tensor_copy(zidx, zof))
            dve.sem_inc(zidx_ready, 1)
            step(ve.tensor_tensor(cnt[:, :], base8[:, :], eoff, ALU.subtract))
            step(ve.tensor_scalar(nt8, cnt[:, :], float(XT - 1), None, ALU.add))
            step(ve.tensor_scalar(nt8, nt8, 8, None, ALU.logical_shift_right))
            step(ve.tensor_copy(ntf, nt8))
            step(ve.tensor_tensor_scan(cend, ntf, zero8, 0.0, ALU.add, ALU.add))
            step(ve.tensor_copy(cnt[:, :], cend))
            step(ve.tensor_copy(base8[:, :], ntf))
            step(ve.tensor_copy(rank4, rank))
            dve.sem_inc(jidx_ready, 1)
            dve.wait_ge(all_stored, 1)
            dve.wait_ge(jidx_ready, 1)
            step(ve.tensor_tensor_scan(jidx, one8[:, :].broadcast_to([P, NT]), zcol[:, :].broadcast_to([P, NT]), -1.0, ALU.add,
                                       ALU.add))
            step(ve.tensor_tensor(tge, cnt[:, :].unsqueeze(1).broadcast_to([P, NT, E]),
                                  jidx.unsqueeze(2).broadcast_to([P, NT, E]), ALU.is_le))
            step(ve.tensor_reduce(tej, tge, AX.X, ALU.add))
            step(ve.tensor_tensor(tgn, tge, base8[:, :].unsqueeze(1).broadcast_to([P, NT, E]), ALU.mult))
            step(ve.tensor_reduce(tst, tgn, AX.X, ALU.add))
            step(ve.tensor_tensor(tst, jidx, tst, ALU.subtract))
            step(ve.tensor_scalar(tst, tst, float(XT), None, ALU.mult))
            step(ve.scalar_tensor_tensor(tab[:, 1, :], tej, float(R), tst, ALU.mult, ALU.add))
            step(ve.tensor_scalar(tab[:, 0, :], tej, float(E - 1), None, ALU.min))
            dve.sem_inc(tab_ready, 1)
            step(ve.tensor_tensor(start, cnt[:, :], base8[:, :], ALU.subtract))
            step(ve.tensor_scalar(start, start, float(XT), None, ALU.mult))
            row = slots[:, :, :].rearrange("p r t -> p (r t)")
            step(ve.tensor_scalar(which, row, RB, None, ALU.logical_shift_right))
            step(ve.tensor_scalar(whichf, which, -1.0, float(E), ALU.mult, ALU.add))
            step(ve.tensor_scalar(row, row, R - 1, None, ALU.bitwise_and))
            step(ve.tensor_tensor(chosen, whichf.unsqueeze(2).broadcast_to([P, 2 * T, E]),
                                  rank4.unsqueeze(1).broadcast_to([P, 2 * T, E]), ALU.is_equal))
            step(ve.tensor_tensor(chosen, chosen, start.unsqueeze(1).broadcast_to([P, 2 * T, E]), ALU.mult))
            step(ve.tensor_reduce(whichf, chosen, AX.X, ALU.add))
            step(ve.tensor_tensor(row, row, whichf, ALU.add))
            end4 = did.base + did.n

            def pair_of_tiles(i, first):
                e = [dve.value_load(tab[0:1, 0, ds(2 * i + k, 1)], min_val=0, max_val=E - 1) for k in range(2)]
                for k in range(2):
                    j = 2 * i + k
                    dve.wait_ge(xt4_ready, j + 1)
                    if not first:
                        dve.wait_ge(h_ready, j - 1)
                    ve.tensor_copy(xT[:, k, 1, :, :].rearrange("p a b -> p (a b)"),
                                   bank[6 + k][:, :].bitcast(f16)[:, 0:2 * XT]).then_inc(xt4_lo, 1)
                for k in range(2):
                    j = 2 * i + k
                    dve.wait_ge(gelu_ready, j + 1)
                    if not first:
                        dve.wait_ge(y_ready, j - 1)
                    ve.tensor_copy(hh[:, k, :, :], h32[:, k, :, :]).then_inc(hh_ready, 1)
                    dve.wait_ge(hh_ready, j + 1)
                    ve.tensor_tensor(hl[:, k, :, :], h32[:, k, :, :], hh[:, k, :, :],
                                     ALU.subtract).then_inc(hl_ready, 1)
                for k in range(2):
                    j = 2 * i + k
                    dve.wait_ge(y_ready, j + 1)
                    if not first:
                        dve.wait_ge(y_stored[k], 16 * i)
                    bias = b2s[:, ds(e[k], 1), :].broadcast_to([P, 2, D])
                    ve.scalar_tensor_tensor(yb[:, k, :, :], bank[4 + k][:, :].rearrange("p (h d) -> p h d", h=2),
                                            1.0 / SCALE, bias, ALU.mult, ALU.add).then_inc(y_taken, 1)

            pair_of_tiles(0, True)
            with dve.Fori(1, NT // 2) as i:
                pair_of_tiles(i, False)

            dve.wait_ge(experts_done, 1)

            def give_slots(b, k, base):
                did.start(base)
                did.done(ve.tensor_copy(yidx[:, k, :, :], slots[:, :, ds(b * B, B)]))
                did.settle()
                dve.sem_inc(yidx_ready, 1)

            def result_batch(b, k, i, ahead, base):
                did.start(base)
                dve.wait_ge(yg_full[k], 16 * 2 * B * i + 16 * 2 * B)
                for r in range(2):
                    for s in range(B):
                        t = b * B + s
                        xt_ = xs[:, ds(t, 1), :].rearrange("p a d -> p (a d)")
                        did.done(ve.scalar_tensor_tensor(xt_, yg[:, k, r, s, :], comb[:, r, ds(t, 1)], xt_, ALU.mult,
                                                         ALU.add))
                    did.settle()
                dve.sem_inc(out_ready, 1)
                if ahead:
                    give_slots(b + 2, k, base + 2 * B)

            give_slots(0, 0, end4)
            give_slots(1, 1, end4 + 1)
            start5 = end4 + 2
            with dve.Fori(0, NB // 2 - 1) as i:
                for k in range(2):
                    result_batch(2 * i + k, k, i, True, start5 + (2 * i + k) * (2 * B + 1))
            for k in range(2):
                result_batch(NB - 2 + k, k, NB // 2 - 1, False, start5 + (NB - 2) * (2 * B + 1) + k * 2 * B)


def kernel(x, src, dst, L0_gnn_W, L0_gnn_b, L0_ffn_router_w, L0_ffn_w1, L0_ffn_b1, L0_ffn_w2, L0_ffn_b2):
    import numpy as np
    import concourse.bacc as bacc
    from concourse import mybir as mb
    from concourse.bass_utils import run_bass_kernel_spmd

    src, dst = np.asarray(src), np.asarray(dst)
    s, d = src.reshape(NCH, CH), dst.reshape(NCH, CH)
    arrays = {
        "x": np.asarray(x),
        "src_cols": s.T,
        "edge_rows": np.concatenate([s, d], axis=1),
        "wg": np.asarray(L0_gnn_W).reshape(D, 2, 2, P).transpose(3, 2, 1, 0).reshape(P, 4 * D),
        "bg": np.asarray(L0_gnn_b),
        "rw": np.asarray(L0_ffn_router_w).reshape(E, 2, P).transpose(2, 1, 0).reshape(P, 2 * E),
        "w1": np.asarray(L0_ffn_w1),
        "b1": np.asarray(L0_ffn_b1).reshape(E, 2, P).transpose(2, 0, 1).reshape(P, 2 * E),
        "w2": np.asarray(L0_ffn_w2),
        "b2": np.asarray(L0_ffn_b2),
    }
    arrays = {k: np.ascontiguousarray(v) for k, v in arrays.items()}
    nc = bacc.Bacc("TRN2", target_bir_lowering=False, num_devices=1)
    args = [nc.dram_tensor(k, v.shape, mb.dt.from_np(v.dtype), kind="ExternalInput").ap() for k, v in arrays.items()]
    out = nc.dram_tensor("out", (N, D), mb.dt.float32, kind="ExternalOutput").ap()
    gnn_moe(nc, *args, out)
    return run_bass_kernel_spmd(nc, [arrays], core_ids=[0]).results[0]["out"]
```

```python
import concourse.bass as bass
from concourse import mybir
from concourse.alu_op_type import AluOpType as ALU
from contextlib import ExitStack

P = 128
N = 12500
D = 256
E = 8
EDGES = 200000
T = (N + P - 1) // P
TAIL = N - (T - 1) * P
NP = T * P
CH = 125
NCH = EDGES // CH
GC = 32
NG = NCH // GC
BITS = 7
EXP0 = 15
H1, H2 = 4, 25
TP = H1 * H2
assert TP >= T
KEY = 16384
B = 7
NB = T // B
XT = 256
RB = 14
R = 1 << RB
assert R >= NP + XT
NT = (2 * NP + E * (XT - 1)) // XT + 1
DUMMY = NT - 2 * NP // XT
ROWS = E * R + DUMMY * XT
SCALE = 64.0
EPS = 1e-5


class Count:

    def __init__(self, eng, sem):
        self.eng, self.sem, self.base, self.n = eng, sem, 0, 0

    def start(self, base):
        self.base, self.n = base, 0

    def done(self, instruction):
        instruction.then_inc(self.sem, 1)
        self.n += 1

    def settle(self):
        self.eng.wait_ge(self.sem, self.base + self.n)


def gnn_moe(nc, x, src_cols, edge_rows, wg, bg, rw, w1, b1, w2, b2, out):
    f32, f16, bf16, i32, u8 = (mybir.dt.float32, mybir.dt.float16, mybir.dt.bfloat16, mybir.dt.int32,
                               mybir.dt.uint8)
    ACT = mybir.ActivationFunctionType
    AX = mybir.AxisListType
    ds = bass.ds
    SIZE = {f32: 4, i32: 4, f16: 2, bf16: 2}

    agg_rows = nc.dram_tensor("agg_rows", [NP + P, D], f32).ap()
    tok_rows = nc.dram_tensor("tok_rows", [ROWS, 2 * D], f16).ap()
    y_rows = nc.dram_tensor("y_rows", [NT * XT, D], f32).ap()

    ctx = ExitStack()
    with ctx:
        def sb(name, shape, dt):
            return ctx.enter_context(nc.sbuf_tensor(name, shape, dt))

        def sem(name):
            return ctx.enter_context(nc.semaphore(name))

        xs = sb("xs", [P, T, D], f32)
        w1s = sb("w1s", [P, 2, E, 2, D], f16)
        w2s = sb("w2s", [P, 2, E, 2, D], f16)
        wgs = sb("wgs", [P, 2, 2, 2 * D], f16)
        rws = sb("rws", [P, 2, E], f32)
        b1s = sb("b1s", [P, E, 2], f32)
        bgs = sb("bgs", [P, D], f32)
        ident = sb("ident", [P, P], f32)
        identh = sb("identh", [P, P], f16)
        mv = sb("mv", [P, T, 2], f32)
        rstd = sb("rstd", [P, T], f32)
        nmr = sb("nmr", [P, T], f32)
        mvb = sb("mvb", [P, B, 2], f32)
        bst3 = sb("bst3", [P, B, 6], f32)
        base8 = sb("base8", [P, E], f32)
        rank4 = sb("rank4", [P, E], f32)[:, :]
        one8 = sb("one8", [P, 1], f32)
        zcol = sb("zcol", [P, 1], f32)
        eps = sb("eps", [P, 1], f32)
        cid = sb("cid", [P, T], i32)
        nid = sb("nid", [P, T], f32)
        gat = sb("gat", [P, T], i32)
        slots = sb("slots", [P, 2, T], i32)
        comb = sb("comb", [P, 2, T], f32)
        cnt = sb("cnt", [P, E], f32)
        tab = sb("tab", [P, 2, NT], i32)

        arena_bytes = 66944
        arena = sb("arena", [P, arena_bytes], u8)

        class Arena:
            def __init__(self):
                self.at = 0

            def take(self, shape, dt):
                n = SIZE[dt]
                for s in shape[1:]:
                    n *= s
                a = arena[0:shape[0], self.at:self.at + n].bitcast(dt)
                self.at += (n + 31) // 32 * 32
                assert self.at <= arena_bytes, self.at
                names = "abcd"[:len(shape) - 1]
                if len(names) > 1:
                    a = a.rearrange(f"p ({' '.join(names)}) -> p {' '.join(names)}",
                                    **{k: s for k, s in zip(names, shape[1:])})
                return a

        one = Arena()
        lo7 = one.take([CH, NCH], bf16)
        hi1 = one.take([CH, NCH], bf16)
        hi2 = one.take([CH, NCH], bf16)
        oh_lo = one.take([CH, 2, GC // 2, P, 2], bf16)
        oh_hi = one.take([CH, GC // 2, TP, 2], bf16)
        oh_1 = one.take([CH, GC // 2, H1, 2], bf16)
        oh_2 = one.take([CH, GC // 2, H2, 2], bf16)
        weigh = one.take([CH, GC // 2, H1, 2], bf16)
        vbuf = one.take([P, NG, T], i32)
        iota = one.take([P, P, 2], bf16)
        xn = one.take([P, 2, D], f32)
        xh = one.take([P, 2, D], f16)
        xl = one.take([P, 2, D], f16)
        pb = one.take([P, 2, D], f32)
        sf = one.take([P, 2, D], f32)
        wst = one.take([P, 2, D], f32)
        onesh = one.take([P, P], f16)
        brow = one.take([P, D], f16)
        bpart = xn[0:1, :, :].rearrange("p a d -> p (a d)").bitcast(f16)[:, 0:3 * D].rearrange("p (n d) -> p n d", d=D)
        brest = pb[0:1, 0, :]
        srcs = vbuf[0:CH, 0:17, :].rearrange("p a b -> p (a b)")[:, 0:NCH]
        part = vbuf[0:CH, 17:34, :].rearrange("p a b -> p (a b)")[:, 0:NCH]
        wgf = vbuf[:, 34:45, :].rearrange("p a b -> p (a b)")[:, 0:4 * D].bitcast(f32)
        fbuf = Arena().take([P, NG, T], f32)

        two = Arena()
        g256 = one.take([P, NG], f32)
        er = two.take([P, 2, B, 2 * CH], i32)
        two.at = max(two.at, 33000)
        kcode = two.take([P, CH], f32)
        ekey = two.take([P, B, CH], f32)
        eeq = two.take([P, B, CH], f32)
        wm = two.take([P, B], f32)
        wmi = two.take([P, B], i32)
        wabs = two.take([P, B], f32)
        cst = two.take([P, 2, B], i32)

        three = Arena()
        pg = three.take([P, 2, B, D], f32)
        thl = three.take([P, 2, B, 2 * D], f16)
        t32 = three.take([P, B, D], f32)
        tT = three.take([P, 2, D], f32)
        tri = three.take([P, P], bf16)
        ones = three.take([P, P], bf16)
        rank = three.take([P, E], f32)
        eoff = three.take([P, E], f32)
        lg = three.take([P, B, E], f32)
        lex = three.take([P, B, E], f32)
        pr = three.take([P, B, E], f32)
        tmp = three.take([P, B, E], f32)
        oh1 = three.take([P, B, E], f32)
        oh2 = three.take([P, B, E], f32)
        msk = three.take([P, B + 1, E], bf16)
        pos = three.take([P, B, E], f32)
        r7 = three.take([P, 8, B], f32)
        sidx = three.take([P, 2, 2, B], i32)
        pidx = three.take([P, 2, B], i32)
        zt = three.take([P, 2 * D], f16)
        zidx = three.take([P, E, 2], i32)
        zof = three.take([P, E, 2], f32)
        nt8 = three.take([P, E], i32)
        ntf = three.take([P, E], f32)
        cend = three.take([P, E], f32)
        zero8 = three.take([P, E], f32)

        four = Arena()
        xd = four.take([P, 2, 2, 2 * D], f16)
        xT = four.take([P, 2, 2, 2, XT], f16)
        h32 = four.take([P, 2, 2, XT], f32)
        hh = four.take([P, 2, 2, XT], f16)
        hl = four.take([P, 2, 2, XT], f16)
        yb = four.take([P, 2, 2, D], f32)
        jidx = four.take([P, NT], f32)
        tge = four.take([P, NT, E], f32)
        tgn = four.take([P, NT, E], f32)
        tej = four.take([P, NT], f32)
        tst = four.take([P, NT], f32)
        assert four.at < 30000 and three.at <= 50000
        four.at = 50000
        b2s = four.take([P, E, D], f32)
        four.at = 30000
        start = four.take([P, E], f32)
        which = four.take([P, 2 * T], i32)
        whichf = four.take([P, 2 * T], f32)
        chosen = four.take([P, 2 * T, E], f32)

        five = Arena()
        yg = five.take([P, 2, 2, B, D], f32)
        yidx = five.take([P, 2, 2, B], i32)

        bank = [ctx.enter_context(nc.psum_tensor(f"bank{i}", [P, 512], f32)) for i in range(8)]

        s_src, s_small, s_wg = sem("s_src"), sem("s_small"), sem("s_wg")
        s_x = [sem(f"s_x{i}") for i in range(NB // 2)]
        s_wst = sem("s_wst")
        w_prep = sem("w_prep")
        zeroed, iota_ready, consts_ready = sem("zeroed"), sem("iota_ready"), sem("consts_ready")
        pool_done, vec_done = sem("pool_done"), sem("vec_done")
        passed, turn = sem("passed"), sem("turn")
        std_ready, ln_ready, var_ready = sem("std_ready"), sem("ln_ready"), sem("var_ready")
        onehots_ready, onehots_used, last_ready, last_taken = (sem("onehots_ready"), sem("onehots_used"),
                                                               sem("last_ready"), sem("last_taken"))
        xn_ready, xt_ready, xh_ready, xl_ready = sem("xn_ready"), sem("xt_ready"), sem("xh_ready"), sem("xl_ready")
        g_ready, self_added, agg_copied, self_copied = (sem("g_ready"), sem("self_added"), sem("agg_copied"),
                                                        sem("self_copied"))
        brow_zeroed, bparts_ready, s_brows, s_b2 = sem("brow_zeroed"), sem("bparts_ready"), sem("s_brows"), sem("s_b2")
        agg_stored = [sem("agg_stored0"), sem("agg_stored1")]
        s_brow = sem("s_brow")
        cid_ready = sem("cid_ready")
        er_full = [sem("er_full0"), sem("er_full1")]
        gat_ready = sem("gat_ready")
        consts3_ready = sem("consts3_ready")
        pidx_ready = sem("pidx_ready")
        pg_full = [sem("pg_full0"), sem("pg_full1")]
        pg_used = sem("pg_used")
        t_ready, tt_ready, ttc_ready, lg_ready = sem("t_ready"), sem("tt_ready"), sem("ttc_ready"), sem("lg_ready")
        tparts_ready = sem("tparts_ready")
        ldiff_ready, lexp_ready, msk_ready, pos_ready, sidx_ready = (sem("ldiff_ready"), sem("lexp_ready"),
                                                                     sem("msk_ready"), sem("pos_ready"),
                                                                     sem("sidx_ready"))
        scattered = [sem("scattered0"), sem("scattered1")]
        zidx_ready, zeros_stored, dummies_stored = sem("zidx_ready"), sem("zeros_stored"), sem("dummies_stored")
        all_stored, tab_ready, jidx_ready, zt_ready = sem("all_stored"), sem("tab_ready"), sem("jidx_ready"), sem("zt_ready")
        xd_full = [sem("xd_full0"), sem("xd_full1")]
        xt4_ready, xt4_hi, xt4_lo, h_ready, gelu_ready, hh_ready, hl_ready, y_ready, y_taken = (
            sem(n) for n in ("xt4_ready", "xt4_hi", "xt4_lo", "h_ready", "gelu_ready", "hh_ready", "hl_ready",
                             "y_ready", "y_taken"))
        y_stored = [sem("y_stored0"), sem("y_stored1")]
        experts_done, yidx_ready = sem("experts_done"), sem("yidx_ready")
        yg_full = [sem("yg_full0"), sem("yg_full1")]
        out_ready, s_out = sem("out_ready"), sem("s_out")

        block = ctx.enter_context(nc.Block())
        x_chunk = T // len(s_x)

        def tokens(a, t, n):
            return a[ds(t * P, n * P), :].rearrange("(s p) d -> p s d", p=P)

        @block.sync
        def _(sp):
            sp.dma_start(srcs, src_cols).then_inc(s_src, 16)
            sp.dma_start(bgs[:, :], bg.rearrange("(a d) -> a d", a=1).broadcast_to([P, D])).then_inc(s_small, 16)
            sp.dma_start(wgf, wg).then_inc(s_wg, 16)
            for c in range(len(s_x)):
                n = x_chunk if c < len(s_x) - 1 else x_chunk - 1
                sp.dma_start(xs[:, c * x_chunk:c * x_chunk + n, :], tokens(x, c * x_chunk, n)).then_inc(s_x[c], 16)
            sp.wait_ge(zeroed, 1)
            sp.dma_start(xs[0:TAIL, T - 1, :], x[(T - 1) * P:N, :]).then_inc(s_x[-1], 16)
            sp.dma_start(rws[:, :, :].rearrange("p a e -> p (a e)"), rw).then_inc(s_small, 16)
            sp.dma_start(b1s[:, :, :].rearrange("p a e -> p (a e)"), b1).then_inc(s_small, 16)
            sp.wait_ge(s_small, 48)
            sp.dma_start(agg_rows[NP:NP + P, :], bgs[:, :]).then_inc(s_brow, 16)

            sp.wait_ge(brow_zeroed, 1)
            sp.wait_ge(bparts_ready, 1)
            for n in range(3):
                sp.dma_start(brow[n:n + 1, :], bpart[:, n, :]).then_inc(s_brows, 16)

            def load_weight(w, e, u, k):
                if u >= 1:
                    sp.wait_ge(w_prep, u)
                sp.dma_start(wst, w[e, :, :].rearrange("(c k) f -> k c f", k=P)).then_inc(s_wst, 16)

            def store_agg(i):
                for k in range(2):
                    sp.wait_ge(agg_copied, 2 * i + k + 1)
                    sp.dma_start(agg_rows[ds((2 * i + k) * P, P), :], pb[:, k, :]).then_inc(agg_stored[k], 16)

            for u in range(2 * E):
                load_weight(w1 if u < E else w2, u % E, u, u % 2)
                store_agg(u)
            with sp.Fori(2 * E, T // 2) as i:
                store_agg(i)

            sp.wait_ge(tab_ready, 1)
            sp.wait_ge(all_stored, 1)

            sp.dma_start(b2s.rearrange("p a e -> p (a e)"),
                         b2.rearrange("e d -> (e d)").rearrange("(a n) -> a n", a=1).broadcast_to([P, E * D])
                         ).then_inc(s_b2, 16)

            def load_tile(j, k):
                row = sp.value_load(tab[0:1, 1, ds(j, 1)], min_val=0, max_val=ROWS - XT)
                sp.dma_start(xd[:, k, :, :],
                             tok_rows[ds(row, XT), :].rearrange("(h p) d -> p h d", p=P)).then_inc(xd_full[k], 16)

            def store_tile(j, k):
                sp.wait_ge(y_taken, j + 1)
                sp.dma_start(y_rows[ds(j * XT, XT), :].rearrange("(h p) d -> p h d", p=P),
                             yb[:, k, :, :]).then_inc(y_stored[k], 16)

            for j in range(2):
                load_tile(j, j)
            for j in range(2):
                sp.wait_ge(xt4_ready, j + 1)
                load_tile(j + 2, j)
            with sp.Fori(0, NT // 2 - 2) as i:
                for k in range(2):
                    sp.wait_ge(xt4_ready, 2 * i + k + 3)
                    load_tile(2 * i + k + 4, k)
                    store_tile(2 * i + k, k)
            for j in range(NT - 4, NT):
                store_tile(j, j % 2)
            for k in range(2):
                sp.wait_ge(y_stored[k], 16 * (NT // 2))
            sp.sem_inc(experts_done, 1)

            with sp.Fori(0, NB - 1) as b:
                sp.wait_ge(out_ready, b + 1)
                sp.dma_start(tokens(out, b * B, B), xs[:, ds(b * B, B), :]).then_inc(s_out, 16)
            sp.wait_ge(out_ready, NB)
            sp.dma_start(tokens(out, (NB - 1) * B, B - 1), xs[:, (NB - 1) * B:T - 1, :]).then_inc(s_out, 16)
            sp.dma_start(out[(T - 1) * P:N, :], xs[0:TAIL, T - 1, :]).then_inc(s_out, 16)
            sp.wait_ge(s_out, 16 * (NB + 1))

        @block.gpsimd
        def _(pool):
            did = Count(pool, pool_done)
            gp = nc.gpsimd
            gp.iota(iota, [[1, P], [0, 2]], 0, 0, allow_small_or_imprecise_dtypes=True).then_inc(iota_ready, 1)
            gp.memset(brow, 0.0).then_inc(brow_zeroed, 1)
            for j in range(GC):
                gp.memset(weigh[:, j // 2, :, j % 2], 2.0 ** (BITS * j + EXP0 - 127)).then_inc(iota_ready, 1)
            gp.memset(onesh, 1.0).then_inc(consts_ready, 1)
            gp.memset(xs[:, T - 1, :], 0.0).then_inc(zeroed, 1)
            gp.memset(one8[:, :], 1.0).then_inc(consts_ready, 1)
            gp.memset(zcol[:, :], 0.0).then_inc(consts_ready, 1)
            gp.memset(eps[:, :], EPS).then_inc(iota_ready, 1)
            gp.iota(g256, [[256, NG]], 0, 0, allow_small_or_imprecise_dtypes=True).then_inc(consts_ready, 1)
            gp.iota(nid[:, :], [[P, T]], 0, 1, allow_small_or_imprecise_dtypes=True).then_inc(consts_ready, 1)
            did.done(gp.memset(ident[:, :], 0.0))
            did.done(gp.memset(identh[:, :], 0.0))
            did.settle()
            for m in (ident, identh):
                gp.affine_select(out=m[:, :], in_=m[:, :], compare_op=ALU.not_equal, fill=1.0, base=0,
                                 pattern=[[-1, P]], channel_multiplier=1).then_inc(consts_ready, 1)

            def prepare_weight(ws, e, u, k):
                pool.wait_ge(s_wst, 16 * (u + 1))
                did.done(gp.tensor_scalar(wst, wst, SCALE, None, ALU.mult))
                did.settle()
                did.done(gp.tensor_copy(ws[:, 0, e, :, :], wst))
                did.settle()
                gp.tensor_tensor(ws[:, 1, e, :, :], wst, ws[:, 0, e, :, :], ALU.subtract).then_inc(w_prep, 1)

            def add_self(i):
                for k in range(2):
                    pool.wait_ge(self_copied, 2 * i + k + 1)
                    xt_ = xs[:, ds(2 * i + k, 1), :].rearrange("p a d -> p (a d)")
                    gp.tensor_tensor(xt_, xt_, sf[:, k, :], ALU.add).then_inc(self_added, 1)

            pool.wait_ge(s_small, 48)
            for u in range(2 * E):
                prepare_weight(w1s if u < E else w2s, u % E, u, u % 2)
                add_self(u)
            with pool.Fori(2 * E, T // 2) as i:
                add_self(i)

            pool.wait_ge(cid_ready, 1)
            gp.iota(kcode, [[KEY, CH]], KEY, 0, allow_small_or_imprecise_dtypes=True).then_inc(consts_ready, 1)

            def gather_edges(b, k):
                pool.wait_ge(cid_ready, b + 2)
                pool.sem_inc(turn, 1)
                for s in range(B):
                    gp.indirect_dma_start(er[:, k, s, :], None, edge_rows,
                                          bass.IndirectOffsetOnAxis(cst[:, k, s:s + 1], 0)).then_inc(er_full[k], 16)

            with pool.Fori(0, NB // 2) as i:
                for k in range(2):
                    gather_edges(2 * i + k, k)

            pool.wait_ge(gat_ready, 1)
            did.done(gp.memset(tri, 1.0))
            did.done(gp.memset(ones, 1.0))
            did.done(gp.memset(msk, 0.0))
            did.done(gp.memset(zero8, 0.0))
            did.done(gp.iota(rank, [[-1, E]], E, 0, allow_small_or_imprecise_dtypes=True))
            did.done(gp.iota(eoff, [[1, E]], 0, 0, allow_small_or_imprecise_dtypes=True))
            did.done(gp.iota(zof, [[0, E], [P, 2]], 0, 1, allow_small_or_imprecise_dtypes=True))
            did.done(gp.memset(zt, 0.0))
            did.settle()
            gp.tensor_scalar(eoff, eoff, float(R), None, ALU.mult).then_inc(consts3_ready, 1)
            gp.affine_select(out=tri, in_=tri, compare_op=ALU.is_gt, fill=0.0, base=0,
                             pattern=[[1, P]], channel_multiplier=-1).then_inc(consts3_ready, 1)
            for j in range(2 * DUMMY):
                pool.dma_start(tok_rows[E * R + j * P:E * R + (j + 1) * P, :], zt).then_inc(dummies_stored, 16)
            for k in range(2):
                pool.wait_ge(agg_stored[k], 16 * (T // 2))
            pool.wait_ge(s_brow, 16)

            def gather_agg(b, k):
                pool.wait_ge(pidx_ready, b + 1)
                pool.sem_inc(turn, 1)
                for s in range(B):
                    gp.indirect_dma_start(pg[:, k, s, :], None, agg_rows,
                                          bass.IndirectOffsetOnAxis(pidx[:, k, s:s + 1], 0)).then_inc(pg_full[k], 16)

            def scatter_tokens(b, k):
                pool.wait_ge(sidx_ready, b + 1)
                pool.sem_inc(turn, 1)
                for s in range(B):
                    for r in range(2):
                        gp.indirect_dma_start(tok_rows, bass.IndirectOffsetOnAxis(sidx[:, k, r, s:s + 1], 0),
                                              thl[:, k, s, :], None).then_inc(scattered[k], 16)

            gather_agg(0, 0)
            with pool.Fori(0, NB // 2 - 1) as i:
                gather_agg(2 * i + 1, 1)
                scatter_tokens(2 * i, 0)
                gather_agg(2 * i + 2, 0)
                scatter_tokens(2 * i + 1, 1)
            gather_agg(NB - 1, 1)
            scatter_tokens(NB - 2, 0)
            scatter_tokens(NB - 1, 1)
            pool.wait_ge(zidx_ready, 1)
            for e in range(E):
                for h in range(2):
                    gp.indirect_dma_start(tok_rows, bass.IndirectOffsetOnAxis(zidx[:, e, h:h + 1], 0),
                                          zt, None).then_inc(zeros_stored, 16)
            for k in range(2):
                pool.wait_ge(scattered[k], 16 * 2 * B * (NB // 2))
            pool.wait_ge(zeros_stored, 16 * 2 * E)
            pool.wait_ge(dummies_stored, 16 * 2 * DUMMY)
            pool.sem_inc(all_stored, 1)
            pool.wait_ge(tab_ready, 1)

            pool.wait_ge(experts_done, 1)

            def gather_results(b, k):
                pool.wait_ge(yidx_ready, b + 1)
                pool.sem_inc(turn, 1)
                for s in range(B):
                    for r in range(2):
                        gp.indirect_dma_start(yg[:, k, r, s, :], None, y_rows,
                                              bass.IndirectOffsetOnAxis(yidx[:, k, r, s:s + 1], 0)
                                              ).then_inc(yg_full[k], 16)

            with pool.Fori(0, NB // 2) as i:
                for k in range(2):
                    gather_results(2 * i + k, k)

        @block.scalar
        def _(act):
            sc = nc.scalar
            act.wait_ge(var_ready, 1)
            act.wait_ge(iota_ready, 2 + GC)
            sc.activation(rstd[:, :], mv[:, :, 1], ACT.Sqrt, bias=eps[:, :]).then_inc(std_ready, 1)
            act.wait_ge(ln_ready, 1)
            act.wait_ge(s_brows, 48)

            def node_pair(i, first):
                for k in range(2):
                    t = 2 * i + k
                    sc.activation(xn[:, k, :], xs[:, ds(t, 1), :].rearrange("p a d -> p (a d)"), ACT.Identity,
                                  bias=nmr[:, ds(t, 1)], scale=rstd[:, ds(t, 1)]).then_inc(xn_ready, 1)
                for k in range(2):
                    act.wait_ge(xt_ready, 2 * i + k + 1)
                    sc.activation(xh[:, k, :], bank[k][:, 0:D], ACT.Copy).then_inc(xh_ready, 1)
                for k in range(2):
                    act.wait_ge(g_ready, 2 * i + k + 1)
                    if not first:
                        act.wait_ge(agg_stored[k], 16 * i)
                    sc.activation(pb[:, k, :], bank[5 + k][:, 0:D], ACT.Copy,
                                  scale=1.0 / SCALE).then_inc(agg_copied, 1)
                    if not first:
                        act.wait_ge(self_added, 2 * i + k - 1)
                    sc.activation(sf[:, k, :], bank[2 + k][:, 0:D], ACT.Copy,
                                  scale=1.0 / SCALE).then_inc(self_copied, 1)

            node_pair(0, True)
            with act.Fori(1, T // 2) as i:
                node_pair(i, False)

            def token_batch(b, k):
                act.wait_ge(var_ready, b + 2)
                sc.activation(rstd[:, ds(b * B, B)], mv[:, ds(b * B, B), 1], ACT.Sqrt,
                              bias=eps[:, :]).then_inc(std_ready, 1)
                act.wait_ge(ln_ready, b + 2)
                for s in range(B):
                    t = b * B + s
                    sc.activation(t32[:, s, :], xs[:, ds(t, 1), :].rearrange("p a d -> p (a d)"), ACT.Identity,
                                  bias=nmr[:, ds(t, 1)], scale=rstd[:, ds(t, 1)]).then_inc(t_ready, 1)
                for s in range(B):
                    act.wait_ge(tt_ready, b * B + s + 1)
                    sc.activation(tT[:, s % 2, :], bank[s % 2][:, 0:D], ACT.Copy).then_inc(ttc_ready, 1)
                act.wait_ge(ldiff_ready, b + 1)
                sc.activation(lex, lg, ACT.Exp).then_inc(lexp_ready, 1)

            with act.Fori(0, NB // 2) as i:
                for k in range(2):
                    token_batch(2 * i + k, k)

            act.wait_ge(tab_ready, 1)

            def take_tokens(j, k, first):
                act.wait_ge(xt4_ready, j + 1)
                if not first:
                    act.wait_ge(h_ready, j - 1)
                sc.activation(xT[:, k, 0, :, :].rearrange("p a b -> p (a b)"),
                              bank[k][:, :].bitcast(f16)[:, 0:2 * XT], ACT.Copy).then_inc(xt4_hi, 1)

            def hidden(j, k, first):
                e = act.value_load(tab[0:1, 0, ds(j, 1)], min_val=0, max_val=E - 1)
                act.wait_ge(h_ready, j + 1)
                if not first:
                    act.wait_ge(hl_ready, j - 1)
                for c in range(2):
                    last = sc.activation(h32[:, k, c, :], bank[2 + k][:, c * XT:(c + 1) * XT], ACT.Gelu,
                                         bias=b1s[:, ds(e, 1), c], scale=1.0 / SCALE)
                last.then_inc(gelu_ready, 1)

            def step_of_two(i, first):
                for k in range(2):
                    take_tokens(2 * i + k + 2, k, False)
                    hidden(2 * i + k + 1, 1 - k, first and k == 0)

            take_tokens(0, 0, True)
            take_tokens(1, 1, True)
            hidden(0, 0, True)
            step_of_two(0, True)
            with act.Fori(1, NT // 2 - 1) as i:
                step_of_two(i, False)
            hidden(NT - 1, 1, False)

        @block.tensor
        def _(pe):
            mm = nc.tensor.matmul
            pe.wait_ge(consts_ready, 7)

            def group_of_chunks(g, k, first):
                pe.wait_ge(onehots_ready, g + 1)
                if not first:
                    pe.wait_ge(last_taken, g)
                for c in range(GC):
                    last = mm(bank[4][:, 0:TP], oh_lo[:, k, c // 2, :, c % 2], oh_hi[:, c // 2, :, c % 2],
                              start=(c == 0), stop=(c == GC - 1))
                last.then_inc(onehots_used, 1)

            def node_linear(i, k, first):
                pe.wait_ge(xh_ready, 2 * i + k + 1)
                pe.wait_ge(xl_ready, 2 * i + k + 1)
                if not first:
                    pe.wait_ge(self_copied, 2 * i + k - 1)
                    pe.wait_ge(agg_copied, 2 * i + k - 1)
                n = 0
                for c in range(2):
                    for a, w in ((xh, 0), (xh, 1), (xl, 0)):
                        for to, half in ((bank[2 + k], 0), (bank[5 + k], 1)):
                            mm(to[:, 0:D], a[:, k, c * P:(c + 1) * P], wgs[:, w, c, half * D:(half + 1) * D],
                               start=(n == 0), stop=(n == 5 and half == 0))
                        n += 1
                mm(bank[5 + k][:, 0:D], onesh, brow, start=False, stop=True).then_inc(g_ready, 1)

            def node_pair(i, first):
                for k in range(2):
                    pe.wait_ge(xn_ready, 2 * i + k + 1)
                    if not first:
                        pe.wait_ge(xl_ready, 2 * i + k - 1)
                    for c in range(2):
                        last = nc.tensor.transpose(bank[k][:, c * P:(c + 1) * P], xn[:, k, c * P:(c + 1) * P],
                                                   ident[:, :])
                    last.then_inc(xt_ready, 1)
                node_linear(i, 0, first)
                node_linear(i, 1, first)

            pe.wait_ge(s_brows, 48)
            node_pair(0, True)
            group_of_chunks(0, 0, True)
            node_pair(1, False)
            group_of_chunks(1, 1, False)
            with pe.Fori(1, T // 4) as i:
                for u in range(2):
                    node_pair(2 * i + u, False)
                    group_of_chunks(2 * i + u, u, False)
            node_pair(T // 2 - 1, False)
            for g in range(T // 4 * 2, NG):
                group_of_chunks(g, g % 2, False)

            pe.wait_ge(consts3_ready, 2)

            def token_batch(b, k, first):
                for s in range(B + 1):
                    if s < B:
                        pe.wait_ge(t_ready, b * B + s + 1)
                        if not (first and s < 2):
                            pe.wait_ge(ttc_ready, b * B + s - 1)
                        for c in range(2):
                            last = nc.tensor.transpose(bank[s % 2][:, c * P:(c + 1) * P],
                                                       t32[:, s, c * P:(c + 1) * P], ident[:, :])
                        last.then_inc(tt_ready, 1)
                    if s >= 1:
                        q = s - 1
                        pe.wait_ge(ttc_ready, b * B + q + 1)
                        for c in range(2):
                            last = mm(bank[2][:, q * E:(q + 1) * E], tT[:, q % 2, c * P:(c + 1) * P], rws[:, c, :],
                                      start=(c == 0), stop=(c == 1))
                last.then_inc(lg_ready, 1)
                pe.wait_ge(msk_ready, b + 1)
                places = bank[3][:, 0:(B + 1) * E]
                mm(places, tri, msk.rearrange("p a e -> p (a e)"), start=True, stop=False)
                for s in range(B):
                    n = B - s
                    last = mm(bank[3][:, (s + 1) * E:(B + 1) * E].rearrange("p (a e) -> p a e", e=E), ones,
                              msk[:, s:s + 1, :].broadcast_to([P, n, E]), start=False, stop=(s == B - 1))
                last.then_inc(pos_ready, 1)

            token_batch(0, 0, True)
            token_batch(1, 1, False)
            with pe.Fori(1, NB // 2) as i:
                for k in range(2):
                    token_batch(2 * i + k, k, False)

            pe.wait_ge(tab_ready, 1)
            pe.wait_ge(w_prep, 2 * E)

            def tile_in(i, k, j, first):
                pe.wait_ge(xd_full[k], 16 * i + 16)
                if not first:
                    pe.wait_ge(xt4_hi, j - 1)
                    pe.wait_ge(xt4_lo, j - 1)
                for w in range(2):
                    flip = bank[k + 6 * w][:, :].bitcast(f16)
                    for c in range(2):
                        for h in range(2):
                            at = c * XT + h * P
                            last = nc.tensor.transpose(flip[:, at:at + P],
                                                       xd[:, k, h, w * D + c * P:w * D + (c + 1) * P], identh[:, :])
                last.then_inc(xt4_ready, 1)

            def expert_of(j):
                return pe.value_load(tab[0:1, 0, ds(j, 1)], min_val=0, max_val=E - 1)

            def tile_hidden(j, k, first):
                e = expert_of(j)
                pe.wait_ge(xt4_hi, j + 1)
                pe.wait_ge(xt4_lo, j + 1)
                if not first:
                    pe.wait_ge(gelu_ready, j - 1)
                for f in range(2):
                    n = 0
                    for c in range(2):
                        for w, a in ((0, 0), (0, 1), (1, 0)):
                            last = mm(bank[2 + k][:, f * XT:(f + 1) * XT],
                                      w1s[:, w, ds(e, 1), c, f * P:(f + 1) * P].rearrange("p a f -> p (a f)"),
                                      xT[:, k, a, c, :], start=(n == 0), stop=(n == 5))
                            n += 1
                last.then_inc(h_ready, 1)

            def tile_out(j, k, first):
                e = expert_of(j)
                pe.wait_ge(hh_ready, j + 1)
                pe.wait_ge(hl_ready, j + 1)
                if not first:
                    pe.wait_ge(y_taken, j - 1)
                for h in range(2):
                    n = 0
                    for c in range(2):
                        for a, w in ((hh, 0), (hh, 1), (hl, 0)):
                            last = mm(bank[4 + k][:, h * D:(h + 1) * D], a[:, k, c, h * P:(h + 1) * P],
                                      w2s[:, w, ds(e, 1), c, :].rearrange("p a d -> p (a d)"),
                                      start=(n == 0), stop=(n == 5))
                            n += 1
                last.then_inc(y_ready, 1)

            def step_of_two(i, first):
                for k in range(2):
                    j = 2 * i + k
                    tile_in(i + 1, k, j + 2, False)
                    tile_hidden(j + 1, 1 - k, first and k == 0)
                    tile_out(j, k, first)

            tile_in(0, 0, 0, True)
            tile_in(0, 1, 1, True)
            tile_hidden(0, 0, True)
            step_of_two(0, True)
            with pe.Fori(1, NT // 2 - 1) as i:
                step_of_two(i, False)
            tile_hidden(NT - 1, 1, False)
            tile_out(NT - 2, 0, False)
            tile_out(NT - 1, 1, False)

        @block.vector
        def _(dve):
            ve = nc.vector
            did = Count(dve, vec_done)

            def step(instruction):
                did.done(instruction)
                did.settle()

            dve.wait_ge(s_src, 16)
            step(ve.tensor_scalar(part, srcs, P - 1, None, ALU.bitwise_and))
            step(ve.tensor_copy(lo7, part))
            step(ve.tensor_scalar(srcs, srcs, 7, None, ALU.logical_shift_right))
            step(ve.tensor_scalar(part, srcs, 41.0, None, ALU.mult))
            step(ve.tensor_scalar(part, part, 10, None, ALU.logical_shift_right))
            did.done(ve.tensor_copy(hi1, part))
            did.done(ve.scalar_tensor_tensor(hi2, part, -float(H2), srcs, ALU.mult, ALU.add))
            dve.wait_ge(s_small, 48)
            step(ve.tensor_scalar(brest, bgs[0:1, :], SCALE, None, ALU.mult))
            for n in range(3):
                step(ve.tensor_copy(bpart[:, n, :], brest))
                if n < 2:
                    step(ve.tensor_tensor(brest, brest, bpart[:, n, :], ALU.subtract))
            dve.sem_inc(bparts_ready, 1)
            dve.wait_ge(s_wg, 16)
            did.done(ve.tensor_scalar(wgf, wgf, SCALE, None, ALU.mult))
            did.settle()
            did.done(ve.tensor_copy(wgs[:, 0, :, :].rearrange("p a b -> p (a b)"), wgf))
            did.settle()
            did.done(ve.tensor_tensor(wgs[:, 1, :, :].rearrange("p a b -> p (a b)"), wgf,
                                      wgs[:, 0, :, :].rearrange("p a b -> p (a b)"), ALU.subtract))
            first_stats = did.n
            def layer_statistics(b):
                for s in range(B):
                    did.done(ve.bn_stats(bst3[:, s, :], xs[:, ds(b * B + s, 1), :].rearrange("p a d -> p (a d)")))
                did.settle()
                dve.sem_inc(passed, 1)
                for s in range(B):
                    did.done(ve.bn_aggr(mvb[:, s, :], bst3[:, s, :]))
                did.settle()
                did.done(ve.tensor_copy(mv[:, ds(b * B, B), :], mvb[:, :, :]))

            per = 2 * B + 1
            for c in range(len(s_x)):
                dve.wait_ge(s_x[c], 16 if c < len(s_x) - 1 else 32)
                for k in range(2):
                    did.start(first_stats + (2 * c + k) * per)
                    layer_statistics(2 * c + k)
            did.settle()
            dve.sem_inc(var_ready, 1)
            dve.wait_ge(std_ready, 1)
            did.done(ve.reciprocal(rstd[:, :], rstd[:, :]))
            did.settle()
            ve.scalar_tensor_tensor(nmr[:, :], mv[:, :, 0], -1.0, rstd[:, :], ALU.mult, ALU.mult).then_inc(ln_ready, 1)
            before = did.base + did.n

            dve.wait_ge(iota_ready, 2 + GC)
            dve.wait_ge(consts_ready, 7)

            def pairs(table, g):
                return table[:, ds(g * GC, GC)].rearrange("p (c q) -> p c q", q=2).unsqueeze(2)

            def low_onehots(g, k, first):
                if not first:
                    dve.wait_ge(onehots_used, g - 1)
                ve.tensor_tensor(oh_lo[:, k, :, :, :], iota[0:CH, :, :].unsqueeze(1).broadcast_to([CH, GC // 2, P, 2]),
                                 pairs(lo7, g).broadcast_to([CH, GC // 2, P, 2]), ALU.is_equal)

            def high_onehots(g, first):
                if not first:
                    dve.wait_ge(onehots_ready, g)
                did.done(ve.tensor_tensor(oh_1, iota[0:CH, 0:H1, :].unsqueeze(1).broadcast_to([CH, GC // 2, H1, 2]),
                                          pairs(hi1, g).broadcast_to([CH, GC // 2, H1, 2]), ALU.is_equal))
                did.done(ve.tensor_tensor(oh_2, iota[0:CH, 0:H2, :].unsqueeze(1).broadcast_to([CH, GC // 2, H2, 2]),
                                          pairs(hi2, g).broadcast_to([CH, GC // 2, H2, 2]), ALU.is_equal))
                did.settle()
                did.done(ve.tensor_tensor(oh_1, oh_1, weigh, ALU.mult))
                did.settle()
                if not first:
                    dve.wait_ge(onehots_used, g)
                for a in range(H1):
                    last = ve.tensor_tensor(oh_hi[:, :, a * H2:(a + 1) * H2, :], oh_2,
                                            oh_1[:, :, a:a + 1, :].broadcast_to([CH, GC // 2, H2, 2]), ALU.mult)
                last.then_inc(onehots_ready, 1)

            def take_group(g):
                dve.wait_ge(onehots_used, g + 1)
                ve.tensor_scalar(vbuf[:, ds(g, 1), :].rearrange("p a t -> p (a t)"), bank[4][:, 0:T].bitcast(i32), 23,
                                 None, ALU.logical_shift_right).then_inc(last_taken, 1)

            def low_tokens(i):
                for k in range(2):
                    dve.wait_ge(xh_ready, 2 * i + k + 1)
                    ve.tensor_tensor(xl[:, k, :], bank[k][:, 0:D], xh[:, k, :], ALU.subtract).then_inc(xl_ready, 1)

            def group(g, k, tiles):
                did.start(before + 3 * g)
                low_onehots(g, k, isinstance(g, int) and g < 2)
                if not (isinstance(g, int) and g == 0):
                    take_group(g - 1)
                if tiles:
                    if not (isinstance(g, int) and g == 0):
                        dve.wait_ge(g_ready, 2 * g)
                    low_tokens(g)
                high_onehots(g, isinstance(g, int) and g == 0)

            group(0, 0, True)
            group(1, 1, True)
            with dve.Fori(1, T // 4) as i:
                for k in range(2):
                    group(2 * i + k, k, True)
            for g in range(T // 4 * 2, NG):
                group(g, g % 2, g < T // 2)
            take_group(NG - 1)
            dve.wait_ge(last_taken, NG)

            step(ve.scalar_tensor_tensor(fbuf, vbuf, 0.0, g256[:, :].unsqueeze(2).broadcast_to([P, NG, T]), ALU.is_gt,
                                         ALU.mult))
            step(ve.tensor_tensor(fbuf, fbuf, vbuf, ALU.add))
            step(ve.tensor_reduce(rstd[:, :], fbuf.rearrange("p g t -> p t g"), AX.X, ALU.max))
            group, field = gat, slots[:, 0, :]
            step(ve.tensor_copy(cid[:, :], rstd[:, :]))
            step(ve.tensor_scalar(group[:, :], cid[:, :], 8, None, ALU.logical_shift_right))
            step(ve.tensor_scalar(field, cid[:, :], 255, None, ALU.bitwise_and))
            step(ve.tensor_scalar(nmr[:, :], field, float(EXP0), 0.0, ALU.subtract, ALU.max))
            step(ve.tensor_scalar(field, nmr[:, :], 293.0, None, ALU.mult))
            step(ve.tensor_scalar(field, field, 11, None, ALU.logical_shift_right))
            step(ve.scalar_tensor_tensor(cid[:, :], group[:, :], float(GC), field, ALU.mult, ALU.add))
            dve.sem_inc(cid_ready, 1)
            before2 = did.base + did.n
            PER2 = 9

            def give_chunks(b, k):
                ve.tensor_copy(cst[:, k, :], cid[:, ds(b * B, B)]).then_inc(cid_ready, 1)

            def edge_batch(b, k, i, ahead):
                dve.wait_ge(er_full[k], 16 * B * i + 16 * B)
                did.done(ve.tensor_tensor(ekey, er[:, k, :, CH:2 * CH],
                                          kcode.unsqueeze(1).broadcast_to([P, B, CH]), ALU.add))
                did.done(ve.tensor_tensor(eeq, er[:, k, :, 0:CH],
                                          nid[:, ds(b * B, B)].unsqueeze(2).broadcast_to([P, B, CH]), ALU.is_equal))
                did.settle()
                if ahead:
                    give_chunks(b + 2, k)
                step(ve.tensor_tensor(eeq, eeq, ekey, ALU.mult))
                step(ve.tensor_reduce(wm, eeq, AX.X, ALU.max))
                did.done(ve.tensor_copy(wmi, wm))
                did.done(ve.tensor_scalar(wabs, wm, 0.0, float(NP), ALU.is_equal, ALU.mult))
                did.settle()
                step(ve.tensor_scalar(wmi, wmi, KEY - 1, None, ALU.bitwise_and))
                step(ve.tensor_tensor(gat[:, ds(b * B, B)], wmi, wabs, ALU.add))

            dve.wait_ge(consts_ready, 8)
            did.start(before2)
            give_chunks(0, 0)
            give_chunks(1, 1)
            with dve.Fori(0, NB // 2 - 1) as i:
                for k in range(2):
                    did.start(before2 + (2 * i + k) * (PER2 - 1))
                    edge_batch(2 * i + k, k, i, True)
            for k in range(2):
                did.start(before2 + (NB - 2 + k) * (PER2 - 1))
                edge_batch(NB - 2 + k, k, NB // 2 - 1, False)
            assert did.n == PER2 - 1
            before3 = did.base + did.n
            dve.sem_inc(gat_ready, 1)
            dve.wait_ge(consts3_ready, 2)

            def give_rows(b, k):
                did.done(ve.tensor_copy(pidx[:, k, :], gat[:, ds(b * B, B)]))
                did.settle()
                dve.sem_inc(pidx_ready, 1)

            def token_batch(b, k, i, first, ahead):
                def bc(a):
                    return a.unsqueeze(2).broadcast_to([P, B, E])

                if ahead:
                    give_rows(b + 1, 1 - k)
                else:
                    did.n += 1
                dve.wait_ge(pg_full[k], 16 * B * i + 16 * B)
                xb = xs[:, ds(b * B, B), :]
                step(ve.tensor_tensor(xb, xb, pg[:, k, :, :], ALU.add))
                dve.sem_inc(passed, 1)
                layer_statistics(b)
                did.settle()
                dve.sem_inc(var_ready, 1)
                dve.wait_ge(std_ready, b + 2)
                rb, nb = rstd[:, ds(b * B, B)], nmr[:, ds(b * B, B)]
                step(ve.reciprocal(rb, rb))
                ve.scalar_tensor_tensor(nb, mv[:, ds(b * B, B), 0], -1.0, rb, ALU.mult, ALU.mult).then_inc(ln_ready, 1)
                dve.wait_ge(t_ready, b * B + B)
                if not first:
                    dve.wait_ge(scattered[k], 16 * 2 * B * i)
                hi, lo = thl[:, k, :, 0:D], thl[:, k, :, D:2 * D]
                step(ve.tensor_copy(hi, t32))
                step(ve.tensor_tensor(lo, t32, hi, ALU.subtract))
                step(ve.tensor_tensor(xb, xb, t32, ALU.add))
                dve.wait_ge(lg_ready, b + 1)
                m, q, d, c1, c2 = (r7[:, n, :] for n in range(5))
                logit = bank[2][:, 0:B * E].rearrange("p (a e) -> p a e", e=E)
                step(ve.tensor_reduce(m, logit, AX.X, ALU.max))
                did.done(ve.tensor_tensor(lg, logit, bc(m), ALU.subtract))
                did.settle()
                dve.sem_inc(ldiff_ready, 1)
                dve.wait_ge(lexp_ready, b + 1)
                step(ve.tensor_reduce(q, lex, AX.X, ALU.add))
                step(ve.reciprocal(q, q))
                step(ve.tensor_tensor(pr, lex, bc(q), ALU.mult))
                rk = rank.unsqueeze(1).broadcast_to([P, B, E])

                def pick(top, hot):
                    step(ve.tensor_reduce(top, pr, AX.X, ALU.max))
                    step(ve.tensor_tensor(tmp, pr, bc(top), ALU.is_equal))
                    step(ve.tensor_tensor(tmp, tmp, rk, ALU.mult))
                    step(ve.tensor_reduce(q, tmp, AX.X, ALU.max))
                    step(ve.tensor_tensor(hot, rk, bc(q), ALU.is_equal))

                pick(c1, oh1)
                step(ve.scalar_tensor_tensor(pr, oh1, -2.0, pr, ALU.mult, ALU.add))
                pick(c2, oh2)
                step(ve.tensor_tensor(d, c1, c2, ALU.add))
                step(ve.tensor_scalar(d, d, 1e-12, None, ALU.max))
                step(ve.reciprocal(d, d))
                did.done(ve.tensor_tensor(comb[:, 0, ds(b * B, B)], c1, d, ALU.mult))
                did.done(ve.tensor_tensor(comb[:, 1, ds(b * B, B)], c2, d, ALU.mult))
                did.done(ve.tensor_tensor(msk[:, 0:B, :], oh1, oh2, ALU.add))
                did.settle()
                dve.sem_inc(msk_ready, 1)
                dve.wait_ge(pos_ready, b + 1)
                place = bank[3][:, 0:B * E].rearrange("p (a e) -> p a e", e=E)
                step(ve.tensor_tensor(pos, place, base8[:, :].unsqueeze(1).broadcast_to([P, B, E]), ALU.add))
                for r, hot in ((0, oh1), (1, oh2)):
                    step(ve.tensor_tensor(tmp, hot, pos, ALU.mult))
                    step(ve.tensor_reduce(c1 if r == 0 else c2, tmp, AX.X, ALU.add))
                for r, v in ((0, c1), (1, c2)):
                    did.done(ve.tensor_copy(sidx[:, k, r, :], v))
                    did.done(ve.tensor_copy(slots[:, r, ds(b * B, B)], v))
                did.done(ve.tensor_tensor(base8[:, :], base8[:, :], bank[3][:, B * E:(B + 1) * E], ALU.add))
                did.settle()
                dve.sem_inc(sidx_ready, 1)

            step(ve.tensor_copy(base8[:, :], eoff))
            give_rows(0, 0)
            start3 = before3 + 2
            did.start(start3)
            token_batch(0, 0, 0, True, True)
            PER3 = did.n
            did.start(start3 + PER3)
            token_batch(1, 1, 0, True, True)
            with dve.Fori(1, NB // 2 - 1) as i:
                for k in range(2):
                    did.start(start3 + (2 * i + k) * PER3)
                    token_batch(2 * i + k, k, i, False, True)
            did.start(start3 + (NB - 2) * PER3)
            token_batch(NB - 2, 0, NB // 2 - 1, False, True)
            did.start(start3 + (NB - 1) * PER3 - 1)
            token_batch(NB - 1, 1, NB // 2 - 1, False, False)

            step(ve.tensor_tensor(zof, zof, base8[:, :].unsqueeze(2).broadcast_to([P, E, 2]), ALU.add))
            step(ve.tensor_copy(zidx, zof))
            dve.sem_inc(zidx_ready, 1)
            step(ve.tensor_tensor(cnt[:, :], base8[:, :], eoff, ALU.subtract))
            step(ve.tensor_scalar(nt8, cnt[:, :], float(XT - 1), None, ALU.add))
            step(ve.tensor_scalar(nt8, nt8, 8, None, ALU.logical_shift_right))
            step(ve.tensor_copy(ntf, nt8))
            step(ve.tensor_tensor_scan(cend, ntf, zero8, 0.0, ALU.add, ALU.add))
            step(ve.tensor_copy(cnt[:, :], cend))
            step(ve.tensor_copy(base8[:, :], ntf))
            step(ve.tensor_copy(rank4, rank))
            dve.sem_inc(jidx_ready, 1)
            dve.wait_ge(all_stored, 1)
            dve.wait_ge(jidx_ready, 1)
            step(ve.tensor_tensor_scan(jidx, one8[:, :].broadcast_to([P, NT]), zcol[:, :].broadcast_to([P, NT]), -1.0, ALU.add,
                                       ALU.add))
            step(ve.tensor_tensor(tge, cnt[:, :].unsqueeze(1).broadcast_to([P, NT, E]),
                                  jidx.unsqueeze(2).broadcast_to([P, NT, E]), ALU.is_le))
            step(ve.tensor_reduce(tej, tge, AX.X, ALU.add))
            step(ve.tensor_tensor(tgn, tge, base8[:, :].unsqueeze(1).broadcast_to([P, NT, E]), ALU.mult))
            step(ve.tensor_reduce(tst, tgn, AX.X, ALU.add))
            step(ve.tensor_tensor(tst, jidx, tst, ALU.subtract))
            step(ve.tensor_scalar(tst, tst, float(XT), None, ALU.mult))
            step(ve.scalar_tensor_tensor(tab[:, 1, :], tej, float(R), tst, ALU.mult, ALU.add))
            step(ve.tensor_scalar(tab[:, 0, :], tej, float(E - 1), None, ALU.min))
            dve.sem_inc(tab_ready, 1)
            step(ve.tensor_tensor(start, cnt[:, :], base8[:, :], ALU.subtract))
            step(ve.tensor_scalar(start, start, float(XT), None, ALU.mult))
            row = slots[:, :, :].rearrange("p r t -> p (r t)")
            step(ve.tensor_scalar(which, row, RB, None, ALU.logical_shift_right))
            step(ve.tensor_scalar(whichf, which, -1.0, float(E), ALU.mult, ALU.add))
            step(ve.tensor_scalar(row, row, R - 1, None, ALU.bitwise_and))
            step(ve.tensor_tensor(chosen, whichf.unsqueeze(2).broadcast_to([P, 2 * T, E]),
                                  rank4.unsqueeze(1).broadcast_to([P, 2 * T, E]), ALU.is_equal))
            step(ve.tensor_tensor(chosen, chosen, start.unsqueeze(1).broadcast_to([P, 2 * T, E]), ALU.mult))
            step(ve.tensor_reduce(whichf, chosen, AX.X, ALU.add))
            step(ve.tensor_tensor(row, row, whichf, ALU.add))
            end4 = did.base + did.n

            def take_tokens(j, k, first):
                dve.wait_ge(xt4_ready, j + 1)
                if not first:
                    dve.wait_ge(h_ready, j - 1)
                ve.tensor_copy(xT[:, k, 1, :, :].rearrange("p a b -> p (a b)"),
                               bank[6 + k][:, :].bitcast(f16)[:, 0:2 * XT]).then_inc(xt4_lo, 1)

            def split_hidden(j, k, first):
                dve.wait_ge(gelu_ready, j + 1)
                if not first:
                    dve.wait_ge(y_ready, j - 1)
                ve.tensor_copy(hh[:, k, :, :], h32[:, k, :, :]).then_inc(hh_ready, 1)
                dve.wait_ge(hh_ready, j + 1)
                ve.tensor_tensor(hl[:, k, :, :], h32[:, k, :, :], hh[:, k, :, :], ALU.subtract).then_inc(hl_ready, 1)

            def take_results(i, j, k, first):
                e = dve.value_load(tab[0:1, 0, ds(j, 1)], min_val=0, max_val=E - 1)
                dve.wait_ge(y_ready, j + 1)
                if not first:
                    dve.wait_ge(y_stored[k], 16 * i)
                bias = b2s[:, ds(e, 1), :].broadcast_to([P, 2, D])
                ve.scalar_tensor_tensor(yb[:, k, :, :], bank[4 + k][:, :].rearrange("p (h d) -> p h d", h=2),
                                        1.0 / SCALE, bias, ALU.mult, ALU.add).then_inc(y_taken, 1)

            def step_of_two(i, first):
                for k in range(2):
                    j = 2 * i + k
                    take_tokens(j + 2, k, False)
                    split_hidden(j + 1, 1 - k, first and k == 0)
                    take_results(i, j, k, first)

            take_tokens(0, 0, True)
            take_tokens(1, 1, True)
            split_hidden(0, 0, True)
            dve.wait_ge(s_b2, 16)
            step_of_two(0, True)
            with dve.Fori(1, NT // 2 - 1) as i:
                step_of_two(i, False)
            split_hidden(NT - 1, 1, False)
            take_results(NT // 2 - 1, NT - 2, 0, False)
            take_results(NT // 2 - 1, NT - 1, 1, False)

            dve.wait_ge(experts_done, 1)

            def give_slots(b, k, base):
                did.start(base)
                did.done(ve.tensor_copy(yidx[:, k, :, :], slots[:, :, ds(b * B, B)]))
                did.settle()
                dve.sem_inc(yidx_ready, 1)

            def result_batch(b, k, i, ahead, base):
                did.start(base)
                dve.wait_ge(yg_full[k], 16 * 2 * B * i + 16 * 2 * B)
                for r in range(2):
                    for s in range(B):
                        t = b * B + s
                        xt_ = xs[:, ds(t, 1), :].rearrange("p a d -> p (a d)")
                        did.done(ve.scalar_tensor_tensor(xt_, yg[:, k, r, s, :], comb[:, r, ds(t, 1)], xt_, ALU.mult,
                                                         ALU.add))
                    did.settle()
                dve.sem_inc(out_ready, 1)
                if ahead:
                    give_slots(b + 2, k, base + 2 * B)

            give_slots(0, 0, end4)
            give_slots(1, 1, end4 + 1)
            start5 = end4 + 2
            with dve.Fori(0, NB // 2 - 1) as i:
                for k in range(2):
                    result_batch(2 * i + k, k, i, True, start5 + (2 * i + k) * (2 * B + 1))
            for k in range(2):
                result_batch(NB - 2 + k, k, NB // 2 - 1, False, start5 + (NB - 2) * (2 * B + 1) + k * 2 * B)


def kernel(x, src, dst, L0_gnn_W, L0_gnn_b, L0_ffn_router_w, L0_ffn_w1, L0_ffn_b1, L0_ffn_w2, L0_ffn_b2):
    import numpy as np
    import concourse.bacc as bacc
    from concourse import mybir as mb
    from concourse.bass_utils import run_bass_kernel_spmd

    src, dst = np.asarray(src), np.asarray(dst)
    s, d = src.reshape(NCH, CH), dst.reshape(NCH, CH)
    arrays = {
        "x": np.asarray(x),
        "src_cols": s.T,
        "edge_rows": np.concatenate([s, d], axis=1),
        "wg": np.asarray(L0_gnn_W).reshape(D, 2, 2, P).transpose(3, 2, 1, 0).reshape(P, 4 * D),
        "bg": np.asarray(L0_gnn_b),
        "rw": np.asarray(L0_ffn_router_w).reshape(E, 2, P).transpose(2, 1, 0).reshape(P, 2 * E),
        "w1": np.asarray(L0_ffn_w1),
        "b1": np.asarray(L0_ffn_b1).reshape(E, 2, P).transpose(2, 0, 1).reshape(P, 2 * E),
        "w2": np.asarray(L0_ffn_w2),
        "b2": np.asarray(L0_ffn_b2),
    }
    arrays = {k: np.ascontiguousarray(v) for k, v in arrays.items()}
    nc = bacc.Bacc("TRN2", target_bir_lowering=False, num_devices=1)
    args = [nc.dram_tensor(k, v.shape, mb.dt.from_np(v.dtype), kind="ExternalInput").ap() for k, v in arrays.items()]
    out = nc.dram_tensor("out", (N, D), mb.dt.float32, kind="ExternalOutput").ap()
    gnn_moe(nc, *args, out)
    return run_bass_kernel_spmd(nc, [arrays], core_ids=[0]).results[0]["out"]
```

```python
import concourse.bass as bass
from concourse import mybir
from concourse.alu_op_type import AluOpType as ALU
from contextlib import ExitStack

P = 128
N = 12500
D = 256
E = 8
EDGES = 200000
T = (N + P - 1) // P
TAIL = N - (T - 1) * P
NP = T * P
CH = 125
NCH = EDGES // CH
GC = 32
NG = NCH // GC
BITS = 7
EXP0 = 16
POW0 = 4 * 6
GA = 6
H1, H2 = 4, 25
TP = H1 * H2
assert TP >= T
KEY = 16384
B = 7
NB = T // B
XT = 256
RB = 14
R = 1 << RB
assert R >= NP + XT
NT = (2 * NP + E * (XT - 1)) // XT + 1
DUMMY = NT - 2 * NP // XT
ROWS = E * R + DUMMY * XT
SCALE = 64.0
EPS = 1e-5


class Count:

    def __init__(self, eng, sem):
        self.eng, self.sem, self.base, self.n = eng, sem, 0, 0

    def start(self, base):
        self.base, self.n = base, 0

    def done(self, instruction):
        instruction.then_inc(self.sem, 1)
        self.n += 1

    def settle(self):
        self.eng.wait_ge(self.sem, self.base + self.n)


def gnn_moe(nc, x, src_cols, edge_rows, wg, bg, rw, w1, b1, w2, b2, out):
    f32, f16, bf16, i32, u16, u8 = (mybir.dt.float32, mybir.dt.float16, mybir.dt.bfloat16, mybir.dt.int32, mybir.dt.uint16,
                               mybir.dt.uint8)
    ACT = mybir.ActivationFunctionType
    AX = mybir.AxisListType
    ds = bass.ds
    SIZE = {f32: 4, i32: 4, f16: 2, bf16: 2, u16: 2}

    agg_rows = nc.dram_tensor("agg_rows", [NP + P, D], f32).ap()
    tok_rows = nc.dram_tensor("tok_rows", [ROWS, 2 * D], f16).ap()
    y_rows = nc.dram_tensor("y_rows", [NT * XT, D], f32).ap()

    ctx = ExitStack()
    with ctx:
        def sb(name, shape, dt):
            return ctx.enter_context(nc.sbuf_tensor(name, shape, dt))

        def sem(name):
            return ctx.enter_context(nc.semaphore(name))

        xs = sb("xs", [P, T, D], f32)
        w1s = sb("w1s", [P, 2, E, 2, D], f16)
        w2s = sb("w2s", [P, 2, E, 2, D], f16)
        wgs = sb("wgs", [P, 2, 2, 2 * D], f16)
        rws = sb("rws", [P, 2, E], f32)
        b1s = sb("b1s", [P, E, 2], f32)
        bgs = sb("bgs", [P, D], f32)
        ident = sb("ident", [P, P], f32)
        identh = sb("identh", [P, P], f16)
        mv = sb("mv", [P, T, 2], f32)
        rstd = sb("rstd", [P, T], f32)
        nmr = sb("nmr", [P, T], f32)
        mvb = sb("mvb", [P, B, 2], f32)
        bst3 = sb("bst3", [P, B, 6], f32)
        base8 = sb("base8", [P, E], f32)
        one8 = sb("one8", [P, 1], f32)
        zcol = sb("zcol", [P, 1], f32)
        eps = sb("eps", [P, 1], f32)
        cid = sb("cid", [P, T], i32)
        nid = sb("nid", [P, T], f32)
        gat = sb("gat", [P, T], i32)
        slots = sb("slots", [P, 2, T], i32)
        comb = sb("comb", [P, 2, T], f32)
        cnt = sb("cnt", [P, E], f32)
        tab = sb("tab", [P, 2, NT], i32)
        x32 = sb("x32", [P, 2, D], f32)
        pow2 = sb("pow2", [P, NG], i32)
        kcode = sb("kcode", [P, CH], f32)[:, :]
        tri = sb("tri", [P, P], bf16)[:, :]
        ones = sb("ones", [P, P], bf16)[:, :]
        rank = sb("rank", [P, E], f32)[:, :]
        eoff = sb("eoff", [P, E], f32)[:, :]
        zero8 = sb("zero8", [P, E], f32)[:, :]
        msk = sb("msk", [P, B + 1, E], bf16)[:, :, :]
        zt = sb("zt", [P, 2, 2 * D], f16)
        zrow = sb("zrow", [P, E], i32)
        nt8 = sb("nt8", [P, E], i32)[:, :]
        ntf = sb("ntf", [P, E], f32)[:, :]
        cend = sb("cend", [P, E], f32)[:, :]
        jidx = sb("jidx", [P, NT], f32)[:, :]
        tej = sb("tej", [P, NT], f32)[:, :]
        tst = sb("tst", [P, NT], f32)[:, :]
        start = sb("start", [P, E], f32)[:, :]
        yidx = sb("yidx", [P, 2, 2, B], i32)

        arena_bytes = 60000
        arena = sb("arena", [P, arena_bytes], u8)

        class Arena:
            def __init__(self):
                self.at = 0

            def take(self, shape, dt):
                n = SIZE[dt]
                for s in shape[1:]:
                    n *= s
                a = arena[0:shape[0], self.at:self.at + n].bitcast(dt)
                self.at += (n + 31) // 32 * 32
                assert self.at <= arena_bytes, self.at
                names = "abcd"[:len(shape) - 1]
                if len(names) > 1:
                    a = a.rearrange(f"p ({' '.join(names)}) -> p {' '.join(names)}",
                                    **{k: s for k, s in zip(names, shape[1:])})
                return a

        one = Arena()
        lo7 = one.take([CH, NCH], bf16)
        hi1 = one.take([CH, NCH], bf16)
        hi2 = one.take([CH, NCH], bf16)
        prep = Arena()
        prep.at = one.at
        srcs = prep.take([CH, NCH], i32)
        part = prep.take([CH, NCH], i32)
        wgf = prep.take([P, 4 * D], f32)
        oh_lo = one.take([CH, 2, GC // 2, P, 2], bf16)
        oh_hi = one.take([CH, GC // 2, TP, 2], bf16)
        oh_1 = one.take([CH, GC // 2, H1, 2], bf16)
        oh_2 = one.take([CH, GC // 2, H2, 2], bf16)
        weigh = one.take([CH, GC // 2, H1, 2], bf16)
        vbuf = one.take([P, NG, T], u16)
        iota = one.take([P, P, 2], bf16)
        xn = one.take([P, 2, D], f32)
        xh = one.take([P, 2, D], f16)
        xl = one.take([P, 2, D], f16)
        pb = one.take([P, 2, D], f32)
        sf = one.take([P, 2, D], f32)
        wst = one.take([P, 2, D], f32)
        onesh = one.take([P, P], f16)
        brow = one.take([P, D], f16)
        bpart = xn[0:1, :, :].rearrange("p a d -> p (a d)").bitcast(f16)[:, 0:3 * D].rearrange("p (n d) -> p n d", d=D)
        brest = pb[0:1, 0, :]

        two = Arena()
        er = two.take([P, 2, B, 2 * CH], i32)
        two.at = max(two.at, 33000)
        ekey = two.take([P, B, CH], f32)
        eeq = two.take([P, B, CH], f32)
        wm = two.take([P, B], f32)
        wmi = two.take([P, B], i32)
        wabs = two.take([P, B], f32)
        cst = two.take([P, 2, B], i32)

        three = Arena()
        pg = three.take([P, 2, B, D], f32)
        thl = three.take([P, 2, B, 2 * D], f16)
        t32 = three.take([P, B, D], f32)
        tT = three.take([P, 2, D], f32)
        lg = three.take([P, B, E], f32)
        lex = three.take([P, B, E], f32)
        pr = three.take([P, B, E], f32)
        tmp = three.take([P, B, E], f32)
        oh1 = three.take([P, B, E], f32)
        oh2 = three.take([P, B, E], f32)
        pos = three.take([P, B, E], f32)
        r7 = three.take([P, 8, B], f32)
        sidx = three.take([P, 2, 2, B], i32)
        pidx = three.take([P, 2, B], i32)

        four = Arena()
        xd = four.take([P, 2, 2, 2 * D], f16)
        xT = four.take([P, 2, 2, 2, XT], f16)
        h32 = four.take([P, 2, 2, XT], f32)
        hh = four.take([P, 2, 2, XT], f16)
        hl = four.take([P, 2, 2, XT], f16)
        yb = four.take([P, 2, 2, D], f32)

        four.at = (max(three.at, four.at) + 31) // 32 * 32
        tge = four.take([P, NT, E], f32)
        which = four.take([P, 2 * T], i32)
        whichf = four.take([P, 2 * T], f32)
        chosen = four.take([P, 2 * T, E], f32)
        b2s = four.take([P, E, D], f32)

        five = Arena()
        yg = five.take([P, 2, 2, B, D], f32)

        bank = [ctx.enter_context(nc.psum_tensor(f"bank{i}", [P, 512], f32)) for i in range(8)]

        s_src, s_small, s_wg = sem("s_src"), sem("s_small"), sem("s_wg")
        s_x = [sem(f"s_x{i}") for i in range(NB // 2)]
        s_wst = [sem("s_wst0"), sem("s_wst1")]
        w_prep = sem("w_prep")
        zeroed, iota_ready, consts_ready = sem("zeroed"), sem("iota_ready"), sem("consts_ready")
        pool_done, vec_done = sem("pool_done"), sem("vec_done")
        passed, turn = sem("passed"), sem("turn")
        std_ready, ln_ready, var_ready = sem("std_ready"), sem("ln_ready"), sem("var_ready")
        onehots_ready, onehots_used, last_ready, last_taken = (sem("onehots_ready"), sem("onehots_used"),
                                                               sem("last_ready"), sem("last_taken"))
        xn_ready, xt_ready, xh_ready, xl_ready = sem("xn_ready"), sem("xt_ready"), sem("xh_ready"), sem("xl_ready")
        g_ready, self_added, agg_copied, self_copied = (sem("g_ready"), sem("self_added"), sem("agg_copied"),
                                                        sem("self_copied"))
        brow_zeroed, bparts_ready, s_brows, s_b2 = sem("brow_zeroed"), sem("bparts_ready"), sem("s_brows"), sem("s_b2")
        agg_stored = [sem("agg_stored0"), sem("agg_stored1")]
        s_brow = sem("s_brow")
        cid_ready, scaled, x32_ready = sem("cid_ready"), sem("scaled"), sem("x32_ready")
        er_full = [sem("er_full0"), sem("er_full1")]
        gat_ready = sem("gat_ready")
        consts3_ready = sem("consts3_ready")
        pidx_ready = sem("pidx_ready")
        pg_full = [sem("pg_full0"), sem("pg_full1")]
        pg_used = sem("pg_used")
        t_ready, tt_ready, ttc_ready, lg_ready = sem("t_ready"), sem("tt_ready"), sem("ttc_ready"), sem("lg_ready")
        tparts_ready = sem("tparts_ready")
        ldiff_ready, lexp_ready, msk_ready, pos_ready, sidx_ready = (sem("ldiff_ready"), sem("lexp_ready"),
                                                                     sem("msk_ready"), sem("pos_ready"),
                                                                     sem("sidx_ready"))
        scattered = [sem("scattered0"), sem("scattered1")]
        zrow_ready, zeros_stored, dummies_stored = sem("zrow_ready"), sem("zeros_stored"), sem("dummies_stored")
        tab_ready, zt_ready = sem("tab_ready"), sem("zt_ready")
        xd_full = [sem("xd_full0"), sem("xd_full1")]
        xt4_ready, xt4_hi, xt4_lo, h_ready, gelu_ready, hh_ready, hl_ready, y_ready, y_taken = (
            sem(n) for n in ("xt4_ready", "xt4_hi", "xt4_lo", "h_ready", "gelu_ready", "hh_ready", "hl_ready",
                             "y_ready", "y_taken"))
        y_stored = [sem("y_stored0"), sem("y_stored1")]
        experts_done, yidx_ready = sem("experts_done"), sem("yidx_ready")
        yg_full = [sem("yg_full0"), sem("yg_full1")]
        out_ready, s_out = sem("out_ready"), sem("s_out")

        block = ctx.enter_context(nc.Block())
        x_chunk = T // len(s_x)

        def tokens(a, t, n):
            return a[ds(t * P, n * P), :].rearrange("(s p) d -> p s d", p=P)

        @block.sync
        def _(sp):
            sp.dma_start(srcs, src_cols).then_inc(s_src, 16)
            sp.dma_start(bgs[:, :], bg.rearrange("(a d) -> a d", a=1).broadcast_to([P, D])).then_inc(s_small, 16)
            sp.dma_start(rws[:, :, :].rearrange("p a e -> p (a e)"), rw).then_inc(s_small, 16)
            sp.dma_start(b1s[:, :, :].rearrange("p a e -> p (a e)"), b1).then_inc(s_small, 16)
            sp.dma_start(wgf, wg).then_inc(s_wg, 16)
            for c in range(len(s_x)):
                n = x_chunk if c < len(s_x) - 1 else x_chunk - 1
                sp.dma_start(xs[:, c * x_chunk:c * x_chunk + n, :], tokens(x, c * x_chunk, n)).then_inc(s_x[c], 16)
            sp.wait_ge(zeroed, 1)
            sp.dma_start(xs[0:TAIL, T - 1, :], x[(T - 1) * P:N, :]).then_inc(s_x[-1], 16)
            sp.wait_ge(s_small, 48)
            sp.dma_start(agg_rows[NP:NP + P, :], bgs[:, :]).then_inc(s_brow, 16)

            sp.wait_ge(zt_ready, 1)
            for j in range(DUMMY):
                sp.dma_start(tok_rows[E * R + j * XT:E * R + (j + 1) * XT, :].rearrange("(h p) d -> p h d", p=P),
                             zt[:, :, :]).then_inc(dummies_stored, 16)

            sp.wait_ge(brow_zeroed, 1)
            sp.wait_ge(bparts_ready, 1)
            for n in range(3):
                sp.dma_start(brow[n:n + 1, :], bpart[:, n, :]).then_inc(s_brows, 16)

            def load_weight(w, e, c):
                sp.dma_start(wst[:, c, :], w[ds(e, 1), c * P:(c + 1) * P, :].rearrange("e k f -> k (e f)")
                             ).then_inc(s_wst[c], 16)

            def store_agg(i):
                for k in range(2):
                    sp.wait_ge(agg_copied, 2 * i + k + 1)
                    sp.dma_start(agg_rows[ds((2 * i + k) * P, P), :], pb[:, k, :]).then_inc(agg_stored[k], 16)

            def store_and_load(i, c, w, e):
                store_agg(i)
                sp.wait_ge(w_prep, i + 1)
                load_weight(w, e, c)

            for c in range(2):
                load_weight(w1, 0, c)
            with sp.Fori(0, E - 1) as e:
                for c in range(2):
                    store_and_load(2 * e + c, c, w1, e + 1)
            for c in range(2):
                store_and_load(2 * E - 2 + c, c, w2, 0)
            with sp.Fori(0, E - 1) as e:
                for c in range(2):
                    store_and_load(2 * E + 2 * e + c, c, w2, e + 1)
            with sp.Fori(4 * E - 2, T // 2) as i:
                store_agg(i)

            sp.wait_ge(zrow_ready, 1)
            sp.dma_start(b2s.rearrange("p a e -> p (a e)"),
                         b2.rearrange("e d -> (e d)").rearrange("(a n) -> a n", a=1).broadcast_to([P, E * D])
                         ).then_inc(s_b2, 16)
            sp.wait_ge(dummies_stored, 16 * DUMMY)
            for k in range(2):
                sp.wait_ge(scattered[k], 16 * 2 * B * (NB // 2))
            for e in range(E):
                row = sp.value_load(zrow[0:1, e:e + 1], min_val=0, max_val=E * R - XT)
                sp.dma_start(tok_rows[ds(row, XT), :].rearrange("(h p) d -> p h d", p=P),
                             zt[:, :, :]).then_inc(zeros_stored, 16)
            sp.wait_ge(zeros_stored, 16 * E)
            sp.wait_ge(tab_ready, 1)

            def load_tile(j, k):
                row = sp.value_load(tab[0:1, 1, ds(j, 1)], min_val=0, max_val=ROWS - XT)
                sp.dma_start(xd[:, k, :, :],
                             tok_rows[ds(row, XT), :].rearrange("(h p) d -> p h d", p=P)).then_inc(xd_full[k], 16)

            def store_tile(j, k):
                sp.wait_ge(y_taken, j + 1)
                sp.dma_start(y_rows[ds(j * XT, XT), :].rearrange("(h p) d -> p h d", p=P),
                             yb[:, k, :, :]).then_inc(y_stored[k], 16)

            for j in range(2):
                load_tile(j, j)
            for j in range(2):
                sp.wait_ge(xt4_ready, j + 1)
                load_tile(j + 2, j)
            with sp.Fori(0, NT // 2 - 2) as i:
                for k in range(2):
                    sp.wait_ge(xt4_ready, 2 * i + k + 3)
                    load_tile(2 * i + k + 4, k)
                    store_tile(2 * i + k, k)
            for j in range(NT - 4, NT):
                store_tile(j, j % 2)
            for k in range(2):
                sp.wait_ge(y_stored[k], 16 * (NT // 2))
            sp.sem_inc(experts_done, 1)

            with sp.Fori(0, NB - 1) as b:
                sp.wait_ge(out_ready, b + 1)
                sp.dma_start(tokens(out, b * B, B), xs[:, ds(b * B, B), :]).then_inc(s_out, 16)
            sp.wait_ge(out_ready, NB)
            sp.dma_start(tokens(out, (NB - 1) * B, B - 1), xs[:, (NB - 1) * B:T - 1, :]).then_inc(s_out, 16)
            sp.dma_start(out[(T - 1) * P:N, :], xs[0:TAIL, T - 1, :]).then_inc(s_out, 16)
            sp.wait_ge(s_out, 16 * (NB + 1))

        @block.gpsimd
        def _(pool):
            did = Count(pool, pool_done)
            gp = nc.gpsimd
            gp.iota(iota, [[1, P], [0, 2]], 0, 0, allow_small_or_imprecise_dtypes=True).then_inc(iota_ready, 1)
            gp.memset(brow, 0.0).then_inc(brow_zeroed, 1)
            for j in range(GC):
                gp.memset(weigh[:, j // 2, :, j % 2], 2.0 ** (BITS * j + EXP0 - 127)).then_inc(iota_ready, 1)
            gp.memset(zt[:, :, :], 0.0).then_inc(zt_ready, 1)
            gp.memset(onesh, 1.0).then_inc(consts_ready, 1)
            did.done(gp.iota(pow2[:, :].bitcast(f32), [[1, NG]], POW0 // 4, 0, allow_small_or_imprecise_dtypes=True))
            gp.memset(xs[:, T - 1, :], 0.0).then_inc(zeroed, 1)
            gp.memset(one8[:, :], 1.0).then_inc(consts_ready, 1)
            gp.memset(zcol[:, :], 0.0).then_inc(consts_ready, 1)
            gp.memset(eps[:, :], EPS).then_inc(iota_ready, 1)
            gp.iota(nid[:, :], [[P, T]], 0, 1, allow_small_or_imprecise_dtypes=True).then_inc(consts_ready, 1)
            did.done(gp.memset(ident[:, :], 0.0))
            did.done(gp.memset(identh[:, :], 0.0))
            did.settle()
            gp.tensor_scalar(pow2[:, :], pow2[:, :].bitcast(f32), float(4 << 23), None, ALU.mult).then_inc(consts_ready, 1)
            for m in (ident, identh):
                gp.affine_select(out=m[:, :], in_=m[:, :], compare_op=ALU.not_equal, fill=1.0, base=0,
                                 pattern=[[-1, P]], channel_multiplier=1).then_inc(consts_ready, 1)

            def prepare_weight(ws, e, m, c, base):
                did.start(base)
                pool.wait_ge(s_wst[c], 16 * m + 16)
                pool.sem_inc(turn, 1)
                did.done(gp.tensor_scalar(wst[:, c, :], wst[:, c, :], SCALE, None, ALU.mult))
                did.settle()
                high, low = (ws[:, n, ds(e, 1), c, :].rearrange("p e f -> p (e f)") for n in range(2))
                did.done(gp.tensor_copy(high, wst[:, c, :]))
                did.settle()
                gp.tensor_tensor(low, wst[:, c, :], high, ALU.subtract).then_inc(w_prep, 1)

            def low_tokens(i, first):
                for k in range(2):
                    pool.wait_ge(x32_ready, 2 * i + k + 1)
                    if not first:
                        pool.wait_ge(g_ready, 2 * i + k - 1)
                    gp.tensor_tensor(xl[:, k, :], x32[:, k, :], xh[:, k, :], ALU.subtract).then_inc(xl_ready, 1)

            def add_self(i):
                for k in range(2):
                    pool.wait_ge(self_copied, 2 * i + k + 1)
                    xt_ = xs[:, ds(2 * i + k, 1), :].rearrange("p a d -> p (a d)")
                    gp.tensor_tensor(xt_, xt_, sf[:, k, :], ALU.add).then_inc(self_added, 1)

            gp.iota(kcode, [[KEY, CH]], KEY, 0, allow_small_or_imprecise_dtypes=True).then_inc(consts3_ready, 1)
            did.done(gp.memset(tri, 1.0))
            gp.memset(ones, 1.0).then_inc(consts3_ready, 1)
            gp.memset(msk, 0.0).then_inc(consts3_ready, 1)
            gp.memset(zero8, 0.0).then_inc(consts3_ready, 1)
            gp.iota(rank, [[-1, E]], E, 0, allow_small_or_imprecise_dtypes=True).then_inc(consts3_ready, 1)
            gp.iota(eoff, [[R, E]], 0, 0, allow_small_or_imprecise_dtypes=True).then_inc(consts3_ready, 1)
            did.settle()
            gp.affine_select(out=tri, in_=tri, compare_op=ALU.is_gt, fill=0.0, base=0,
                             pattern=[[1, P]], channel_multiplier=-1).then_inc(consts3_ready, 1)

            pool.wait_ge(s_small, 48)
            low_tokens(0, True)
            before_w = did.n
            for n, ws in ((0, w1s), (2 * E, w2s)):
                with pool.Fori(0, E) as e:
                    for c in range(2):
                        u = 2 * e + (n + c)
                        add_self(u)
                        low_tokens(u + 1, False)
                        prepare_weight(ws, e, e + n // 2, c, before_w + 2 * u)
            with pool.Fori(4 * E, T // 2 - 1) as i:
                add_self(i)
                low_tokens(i + 1, False)
            add_self(T // 2 - 1)

            pool.wait_ge(cid_ready, 1)

            def gather_edges(b, k):
                pool.wait_ge(cid_ready, b + 2)
                pool.sem_inc(turn, 1)
                for s in range(B):
                    gp.indirect_dma_start(er[:, k, s, :], None, edge_rows,
                                          bass.IndirectOffsetOnAxis(cst[:, k, s:s + 1], 0)).then_inc(er_full[k], 16)

            with pool.Fori(0, NB // 2) as i:
                for k in range(2):
                    gather_edges(2 * i + k, k)

            pool.wait_ge(gat_ready, 1)
            for k in range(2):
                pool.wait_ge(agg_stored[k], 16 * (T // 2))
            pool.wait_ge(s_brow, 16)

            def gather_agg(b, k):
                pool.wait_ge(pidx_ready, b + 1)
                pool.sem_inc(turn, 1)
                for s in range(B):
                    gp.indirect_dma_start(pg[:, k, s, :], None, agg_rows,
                                          bass.IndirectOffsetOnAxis(pidx[:, k, s:s + 1], 0)).then_inc(pg_full[k], 16)

            def scatter_tokens(b, k):
                pool.wait_ge(sidx_ready, b + 1)
                pool.sem_inc(turn, 1)
                for s in range(B):
                    for r in range(2):
                        gp.indirect_dma_start(tok_rows, bass.IndirectOffsetOnAxis(sidx[:, k, r, s:s + 1], 0),
                                              thl[:, k, s, :], None).then_inc(scattered[k], 16)

            gather_agg(0, 0)
            gather_agg(1, 1)
            with pool.Fori(0, NB // 2 - 1) as i:
                for k in range(2):
                    gather_agg(2 * i + k + 2, k)
                    scatter_tokens(2 * i + k, k)
            for k in range(2):
                scatter_tokens(NB - 2 + k, k)

            pool.wait_ge(experts_done, 1)

            def gather_results(b, k):
                pool.wait_ge(yidx_ready, b + 1)
                pool.sem_inc(turn, 1)
                for s in range(B):
                    for r in range(2):
                        gp.indirect_dma_start(yg[:, k, r, s, :], None, y_rows,
                                              bass.IndirectOffsetOnAxis(yidx[:, k, r, s:s + 1], 0)
                                              ).then_inc(yg_full[k], 16)

            with pool.Fori(0, NB // 2) as i:
                for k in range(2):
                    gather_results(2 * i + k, k)

        @block.scalar
        def _(act):
            sc = nc.scalar
            def scale_group(g):
                act.wait_ge(last_taken, g + 1)
                v = vbuf[:, ds(g, 1), :].rearrange("p a t -> p (a t)")
                sc.activation(v.bitcast(bf16), v, ACT.Copy, scale=pow2[:, ds(g, 1)].bitcast(f32)).then_inc(scaled, 1)

            SA = GA - 2
            act.wait_ge(iota_ready, 2 + GC)
            act.wait_ge(consts_ready, 7)
            for g in range(SA):
                scale_group(g)
            act.wait_ge(var_ready, 1)
            act.wait_ge(iota_ready, 2 + GC)
            sc.activation(rstd[:, :], mv[:, :, 1], ACT.Sqrt, bias=eps[:, :]).then_inc(std_ready, 1)
            act.wait_ge(ln_ready, 1)
            act.wait_ge(s_brows, 48)

            def normalise(i):
                for k in range(2):
                    t = 2 * i + k
                    sc.activation(xn[:, k, :], xs[:, ds(t, 1), :].rearrange("p a d -> p (a d)"), ACT.Identity,
                                  bias=nmr[:, ds(t, 1)], scale=rstd[:, ds(t, 1)]).then_inc(xn_ready, 1)

            def take_transposed(i, first):
                for k in range(2):
                    act.wait_ge(xt_ready, 2 * i + k + 1)
                    sc.activation(xh[:, k, :], bank[k][:, 0:D], ACT.Copy).then_inc(xh_ready, 1)
                    if not first:
                        act.wait_ge(xl_ready, 2 * i + k - 1)
                    sc.activation(x32[:, k, :], bank[k][:, 0:D], ACT.Copy).then_inc(x32_ready, 1)

            def take_products(i, k, first):
                act.wait_ge(g_ready, 2 * i + k + 1)
                if not first:
                    act.wait_ge(agg_stored[k], 16 * i)
                sc.activation(pb[:, k, :], bank[5 + k][:, 0:D], ACT.Copy, scale=1.0 / SCALE).then_inc(agg_copied, 1)
                if not first:
                    act.wait_ge(self_added, 2 * i + k - 1)
                sc.activation(sf[:, k, :], bank[2 + k][:, 0:D], ACT.Copy, scale=1.0 / SCALE).then_inc(self_copied, 1)

            def pair_step(i, first, ahead, group):
                take_products(i, 0, first)
                if ahead:
                    act.wait_ge(xt_ready, 2 * i + 4)
                    normalise(i + 2)
                take_products(i, 1, first)
                take_transposed(i + 1, False)
                if group:
                    scale_group(i + SA)

            normalise(0)
            take_transposed(0, True)
            normalise(1)
            pair_step(0, True, True, True)
            with act.Fori(1, NG - SA) as i:
                pair_step(i, False, True, True)
            for i in range(NG - SA, T // 2 - 1):
                pair_step(i, False, i < T // 2 - 2, False)
            take_products(T // 2 - 1, 0, False)
            take_products(T // 2 - 1, 1, False)
            def deviations(b):
                act.wait_ge(var_ready, b + 2)
                sc.activation(rstd[:, ds(b * B, B)], mv[:, ds(b * B, B), 1], ACT.Sqrt,
                              bias=eps[:, :]).then_inc(std_ready, 1)

            def tokens_of(b):
                act.wait_ge(ln_ready, b + 2)
                for s in range(B):
                    t = b * B + s
                    sc.activation(t32[:, s, :], xs[:, ds(t, 1), :].rearrange("p a d -> p (a d)"), ACT.Identity,
                                  bias=nmr[:, ds(t, 1)], scale=rstd[:, ds(t, 1)]).then_inc(t_ready, 1)
                for s in range(B):
                    act.wait_ge(tt_ready, b * B + s + 1)
                    sc.activation(tT[:, s % 2, :], bank[s % 2][:, 0:D], ACT.Copy).then_inc(ttc_ready, 1)

            def exponentials(b):
                act.wait_ge(ldiff_ready, b + 1)
                sc.activation(lex, lg, ACT.Exp).then_inc(lexp_ready, 1)

            deviations(0)
            tokens_of(0)
            with act.Fori(0, NB - 1) as b:
                deviations(b + 1)
                exponentials(b)
                tokens_of(b + 1)
            exponentials(NB - 1)

            act.wait_ge(tab_ready, 1)

            def take_tokens(j, k, first):
                act.wait_ge(xt4_ready, j + 1)
                if not first:
                    act.wait_ge(h_ready, j - 1)
                sc.activation(xT[:, k, 0, :, :].rearrange("p a b -> p (a b)"),
                              bank[k][:, :].bitcast(f16)[:, 0:2 * XT], ACT.Copy).then_inc(xt4_hi, 1)

            def hidden(j, k, first):
                e = act.value_load(tab[0:1, 0, ds(j, 1)], min_val=0, max_val=E - 1)
                act.wait_ge(h_ready, j + 1)
                if not first:
                    act.wait_ge(hl_ready, j - 1)
                for c in range(2):
                    last = sc.activation(h32[:, k, c, :], bank[2 + k][:, c * XT:(c + 1) * XT], ACT.Gelu,
                                         bias=b1s[:, ds(e, 1), c], scale=1.0 / SCALE)
                last.then_inc(gelu_ready, 1)

            def step_of_two(i, first):
                for k in range(2):
                    take_tokens(2 * i + k + 2, k, False)
                    hidden(2 * i + k + 1, 1 - k, first and k == 0)

            take_tokens(0, 0, True)
            take_tokens(1, 1, True)
            hidden(0, 0, True)
            step_of_two(0, True)
            with act.Fori(1, NT // 2 - 1) as i:
                step_of_two(i, False)
            hidden(NT - 1, 1, False)

        @block.tensor
        def _(pe):
            mm = nc.tensor.matmul
            pe.wait_ge(consts_ready, 7)

            def group_of_chunks(g, k, first):
                pe.wait_ge(onehots_ready, g + 1)
                if not first:
                    pe.wait_ge(last_taken, g)
                for c in range(GC):
                    last = mm(bank[4][:, 0:TP], oh_lo[:, k, c // 2, :, c % 2], oh_hi[:, c // 2, :, c % 2],
                              start=(c == 0), stop=(c == GC - 1))
                last.then_inc(onehots_used, 1)

            def node_linear(i, k, first):
                pe.wait_ge(xh_ready, 2 * i + k + 1)
                pe.wait_ge(xl_ready, 2 * i + k + 1)
                if not first:
                    pe.wait_ge(self_copied, 2 * i + k - 1)
                    pe.wait_ge(agg_copied, 2 * i + k - 1)
                n = 0
                for c in range(2):
                    for a, w in ((xh, 0), (xh, 1), (xl, 0)):
                        for to, half in ((bank[2 + k], 0), (bank[5 + k], 1)):
                            mm(to[:, 0:D], a[:, k, c * P:(c + 1) * P], wgs[:, w, c, half * D:(half + 1) * D],
                               start=(n == 0), stop=(n == 5 and half == 0))
                        n += 1
                mm(bank[5 + k][:, 0:D], onesh, brow, start=False, stop=True).then_inc(g_ready, 1)

            def node_transposes(i, first):
                for k in range(2):
                    pe.wait_ge(xn_ready, 2 * i + k + 1)
                    if not first:
                        pe.wait_ge(x32_ready, 2 * i + k - 1)
                    for c in range(2):
                        last = nc.tensor.transpose(bank[k][:, c * P:(c + 1) * P], xn[:, k, c * P:(c + 1) * P],
                                                   ident[:, :])
                    last.then_inc(xt_ready, 1)

            def pair_step(i, first):
                node_transposes(i + 1, False)
                node_linear(i, 0, first)
                node_linear(i, 1, first)

            for g in range(GA):
                group_of_chunks(g, g % 2, g == 0)
            pe.wait_ge(s_brows, 48)
            node_transposes(0, True)
            pair_step(0, True)
            group_of_chunks(GA, 0, False)
            pair_step(1, False)
            group_of_chunks(GA + 1, 1, False)
            with pe.Fori(1, (NG - GA) // 2) as i:
                for u in range(2):
                    pair_step(2 * i + u, False)
                    group_of_chunks(2 * i + GA + u, u, False)
            with pe.Fori(NG - GA, T // 2 - 1) as i:
                pair_step(i, False)
            node_linear(T // 2 - 1, 0, False)
            node_linear(T // 2 - 1, 1, False)

            pe.wait_ge(consts3_ready, 7)

            def logits(b, first):
                for s in range(B + 1):
                    if s < B:
                        pe.wait_ge(t_ready, b * B + s + 1)
                        if not (first and s < 2):
                            pe.wait_ge(ttc_ready, b * B + s - 1)
                        for c in range(2):
                            last = nc.tensor.transpose(bank[s % 2][:, c * P:(c + 1) * P],
                                                       t32[:, s, c * P:(c + 1) * P], ident[:, :])
                        last.then_inc(tt_ready, 1)
                    if s >= 1:
                        q = s - 1
                        pe.wait_ge(ttc_ready, b * B + q + 1)
                        for c in range(2):
                            last = mm(bank[2][:, q * E:(q + 1) * E], tT[:, q % 2, c * P:(c + 1) * P], rws[:, c, :],
                                      start=(c == 0), stop=(c == 1))
                last.then_inc(lg_ready, 1)

            def places_of(b):
                pe.wait_ge(msk_ready, b + 1)
                places = bank[3][:, 0:(B + 1) * E]
                mm(places, tri, msk.rearrange("p a e -> p (a e)"), start=True, stop=False)
                for s in range(B):
                    n = B - s
                    last = mm(bank[3][:, (s + 1) * E:(B + 1) * E].rearrange("p (a e) -> p a e", e=E), ones,
                              msk[:, s:s + 1, :].broadcast_to([P, n, E]), start=False, stop=(s == B - 1))
                last.then_inc(pos_ready, 1)

            logits(0, True)
            with pe.Fori(0, NB - 1) as b:
                places_of(b)
                logits(b + 1, False)
            places_of(NB - 1)

            pe.wait_ge(tab_ready, 1)
            pe.wait_ge(w_prep, 4 * E)

            def tile_in(i, k, j, first):
                pe.wait_ge(xd_full[k], 16 * i + 16)
                if not first:
                    pe.wait_ge(xt4_hi, j - 1)
                    pe.wait_ge(xt4_lo, j - 1)
                for w in range(2):
                    flip = bank[k + 6 * w][:, :].bitcast(f16)
                    for c in range(2):
                        for h in range(2):
                            at = c * XT + h * P
                            last = nc.tensor.transpose(flip[:, at:at + P],
                                                       xd[:, k, h, w * D + c * P:w * D + (c + 1) * P], identh[:, :])
                last.then_inc(xt4_ready, 1)

            def expert_of(j):
                return pe.value_load(tab[0:1, 0, ds(j, 1)], min_val=0, max_val=E - 1)

            def tile_hidden(j, k, e, first):
                pe.wait_ge(xt4_hi, j + 1)
                pe.wait_ge(xt4_lo, j + 1)
                if not first:
                    pe.wait_ge(gelu_ready, j - 1)
                for f in range(2):
                    n = 0
                    for c in range(2):
                        for w, a in ((0, 0), (0, 1), (1, 0)):
                            last = mm(bank[2 + k][:, f * XT:(f + 1) * XT],
                                      w1s[:, w, ds(e, 1), c, f * P:(f + 1) * P].rearrange("p a f -> p (a f)"),
                                      xT[:, k, a, c, :], start=(n == 0), stop=(n == 5))
                            n += 1
                last.then_inc(h_ready, 1)

            def tile_out(j, k, e, first):
                pe.wait_ge(hh_ready, j + 1)
                pe.wait_ge(hl_ready, j + 1)
                if not first:
                    pe.wait_ge(y_taken, j - 1)
                n = 0
                for c in range(2):
                    for a, w in ((hh, 0), (hl, 0), (hh, 1)):
                        for h in range(2):
                            last = mm(bank[4 + k][:, h * D:(h + 1) * D], a[:, k, c, h * P:(h + 1) * P],
                                      w2s[:, w, ds(e, 1), c, :].rearrange("p a d -> p (a d)"),
                                      start=(n == 0 and h == 0), stop=(n == 5 and h == 1))
                        n += 1
                last.then_inc(y_ready, 1)

            def step_of_two(i, first):
                e = [expert_of(2 * i), expert_of(2 * i + 1), expert_of(2 * i + 2)]
                for k in range(2):
                    j = 2 * i + k
                    tile_in(i + 1, k, j + 2, False)
                    tile_hidden(j + 1, 1 - k, e[k + 1], first and k == 0)
                    tile_out(j, k, e[k], first)

            tile_in(0, 0, 0, True)
            tile_in(0, 1, 1, True)
            tile_hidden(0, 0, expert_of(0), True)
            step_of_two(0, True)
            with pe.Fori(1, NT // 2 - 1) as i:
                step_of_two(i, False)
            e = [expert_of(NT - 2), expert_of(NT - 1)]
            tile_hidden(NT - 1, 1, e[1], False)
            tile_out(NT - 2, 0, e[0], False)
            tile_out(NT - 1, 1, e[1], False)

        @block.vector
        def _(dve):
            ve = nc.vector
            did = Count(dve, vec_done)

            def step(instruction):
                did.done(instruction)
                did.settle()

            dve.wait_ge(s_src, 16)
            step(ve.tensor_scalar(part, srcs, P - 1, None, ALU.bitwise_and))
            step(ve.tensor_copy(lo7, part))
            step(ve.tensor_scalar(srcs, srcs, 7, None, ALU.logical_shift_right))
            step(ve.tensor_scalar(part, srcs, 41.0, None, ALU.mult))
            step(ve.tensor_scalar(part, part, 10, None, ALU.logical_shift_right))
            did.done(ve.tensor_copy(hi1, part))
            did.done(ve.scalar_tensor_tensor(hi2, part, -float(H2), srcs, ALU.mult, ALU.add))
            dve.wait_ge(s_small, 48)
            step(ve.tensor_scalar(brest, bgs[0:1, :], SCALE, None, ALU.mult))
            for n in range(3):
                step(ve.tensor_copy(bpart[:, n, :], brest))
                if n < 2:
                    step(ve.tensor_tensor(brest, brest, bpart[:, n, :], ALU.subtract))
            dve.sem_inc(bparts_ready, 1)
            dve.wait_ge(s_wg, 16)
            did.done(ve.tensor_scalar(wgf, wgf, SCALE, None, ALU.mult))
            did.settle()
            did.done(ve.tensor_copy(wgs[:, 0, :, :].rearrange("p a b -> p (a b)"), wgf))
            did.settle()
            did.done(ve.tensor_tensor(wgs[:, 1, :, :].rearrange("p a b -> p (a b)"), wgf,
                                      wgs[:, 0, :, :].rearrange("p a b -> p (a b)"), ALU.subtract))
            before = did.n

            def layer_statistics(b):
                for s in range(B):
                    did.done(ve.bn_stats(bst3[:, s, :], xs[:, ds(b * B + s, 1), :].rearrange("p a d -> p (a d)")))
                did.settle()
                dve.sem_inc(passed, 1)
                for s in range(B):
                    did.done(ve.bn_aggr(mvb[:, s, :], bst3[:, s, :]))
                did.settle()
                did.done(ve.tensor_copy(mv[:, ds(b * B, B), :], mvb[:, :, :]))

            dve.wait_ge(iota_ready, 2 + GC)
            dve.wait_ge(consts_ready, 7)

            def pairs(table, g):
                return table[:, ds(g * GC, GC)].rearrange("p (c q) -> p c q", q=2).unsqueeze(2)

            def low_onehots(g, k, first):
                if not first:
                    dve.wait_ge(onehots_used, g - 1)
                ve.tensor_tensor(oh_lo[:, k, :, :, :], iota[0:CH, :, :].unsqueeze(1).broadcast_to([CH, GC // 2, P, 2]),
                                 pairs(lo7, g).broadcast_to([CH, GC // 2, P, 2]), ALU.is_equal)

            def high_onehots(g, first):
                if not first:
                    dve.wait_ge(onehots_ready, g)
                did.done(ve.tensor_tensor(oh_1, iota[0:CH, 0:H1, :].unsqueeze(1).broadcast_to([CH, GC // 2, H1, 2]),
                                          pairs(hi1, g).broadcast_to([CH, GC // 2, H1, 2]), ALU.is_equal))
                did.done(ve.tensor_tensor(oh_2, iota[0:CH, 0:H2, :].unsqueeze(1).broadcast_to([CH, GC // 2, H2, 2]),
                                          pairs(hi2, g).broadcast_to([CH, GC // 2, H2, 2]), ALU.is_equal))
                did.settle()
                did.done(ve.tensor_tensor(oh_1, oh_1, weigh, ALU.mult))
                did.settle()
                if not first:
                    dve.wait_ge(onehots_used, g)
                for a in range(H1):
                    last = ve.tensor_tensor(oh_hi[:, :, a * H2:(a + 1) * H2, :], oh_2,
                                            oh_1[:, :, a:a + 1, :].broadcast_to([CH, GC // 2, H2, 2]), ALU.mult)
                last.then_inc(onehots_ready, 1)

            def take_group(g):
                dve.wait_ge(onehots_used, g + 1)
                sums = bank[4][:, 0:T].bitcast(u16).rearrange("p (t h) -> p t h", h=2)
                ve.tensor_scalar(vbuf[:, ds(g, 1), :].rearrange("p a t -> p (a t)"), sums[:, :, 1], 7, None,
                                  ALU.logical_shift_right).then_inc(last_taken, 1)

            def group(g, k, first, base):
                did.start(base)
                low_onehots(g, k, isinstance(g, int) and g < 2)
                if not first:
                    take_group(g - 1)
                high_onehots(g, first)

            per = 2 * B + 1
            for c in range(len(s_x)):
                if c < GA:
                    group(c, c % 2, c == 0, before)
                    before += 3
                dve.wait_ge(s_x[c], 16 if c < len(s_x) - 1 else 32)
                for k in range(2):
                    did.start(before)
                    layer_statistics(2 * c + k)
                    before += per
            did.settle()
            dve.sem_inc(var_ready, 1)
            dve.wait_ge(std_ready, 1)
            did.done(ve.reciprocal(rstd[:, :], rstd[:, :]))
            did.settle()
            ve.scalar_tensor_tensor(nmr[:, :], mv[:, :, 0], -1.0, rstd[:, :], ALU.mult, ALU.mult).then_inc(ln_ready, 1)
            before += 1

            with dve.Fori(GA // 2, NG // 2) as i:
                for k in range(2):
                    group(2 * i + k, k, False, before + 3 * (2 * i + k - GA))
            did.start(before + 3 * (NG - GA))
            take_group(NG - 1)

            dve.wait_ge(scaled, NG)
            latest, chunk = comb[:, 0, :], comb[:, 1, :]
            step(ve.tensor_reduce(latest, vbuf.bitcast(bf16).rearrange("p g t -> p t g"), AX.X, ALU.max))
            group_of, field = gat, slots[:, 0, :]
            bits = latest.bitcast(i32)
            step(ve.tensor_scalar(group_of[:, :], bits, 25, None, ALU.logical_shift_right))
            step(ve.tensor_scalar(group_of[:, :], group_of[:, :], float((POW0 + 4) // 4), 0.0, ALU.subtract, ALU.max))
            step(ve.tensor_scalar(bits, bits, 0x01FF0000, 128 << 23, ALU.bitwise_and, ALU.bitwise_or))
            step(ve.tensor_scalar(chunk, latest, 8.0, float(EXP0), ALU.mult, ALU.subtract))
            step(ve.tensor_scalar(field, chunk, 293.0, None, ALU.mult))
            step(ve.tensor_scalar(field, field, 11, None, ALU.logical_shift_right))
            step(ve.scalar_tensor_tensor(cid[:, :], group_of[:, :], float(GC), field, ALU.mult, ALU.add))
            dve.sem_inc(cid_ready, 1)
            before2 = did.base + did.n
            PER2 = 9

            def give_chunks(b, k):
                ve.tensor_copy(cst[:, k, :], cid[:, ds(b * B, B)]).then_inc(cid_ready, 1)

            def edge_batch(b, k, i, ahead):
                dve.wait_ge(er_full[k], 16 * B * i + 16 * B)
                did.done(ve.tensor_tensor(ekey, er[:, k, :, CH:2 * CH],
                                          kcode.unsqueeze(1).broadcast_to([P, B, CH]), ALU.add))
                did.done(ve.tensor_tensor(eeq, er[:, k, :, 0:CH],
                                          nid[:, ds(b * B, B)].unsqueeze(2).broadcast_to([P, B, CH]), ALU.is_equal))
                did.settle()
                if ahead:
                    give_chunks(b + 2, k)
                step(ve.tensor_tensor(eeq, eeq, ekey, ALU.mult))
                step(ve.tensor_reduce(wm, eeq, AX.X, ALU.max))
                did.done(ve.tensor_copy(wmi, wm))
                did.done(ve.tensor_scalar(wabs, wm, 0.0, float(NP), ALU.is_equal, ALU.mult))
                did.settle()
                step(ve.tensor_scalar(wmi, wmi, KEY - 1, None, ALU.bitwise_and))
                step(ve.tensor_tensor(gat[:, ds(b * B, B)], wmi, wabs, ALU.add))

            dve.wait_ge(consts3_ready, 7)
            did.start(before2)
            give_chunks(0, 0)
            give_chunks(1, 1)
            with dve.Fori(0, NB // 2 - 1) as i:
                for k in range(2):
                    did.start(before2 + (2 * i + k) * (PER2 - 1))
                    edge_batch(2 * i + k, k, i, True)
            for k in range(2):
                did.start(before2 + (NB - 2 + k) * (PER2 - 1))
                edge_batch(NB - 2 + k, k, NB // 2 - 1, False)
            assert did.n == PER2 - 1
            before3 = did.base + did.n
            dve.sem_inc(gat_ready, 1)
            dve.wait_ge(consts3_ready, 7)

            dve.wait_ge(self_added, 2 * (T // 2))
            def give_rows(b, k):
                did.done(ve.tensor_copy(pidx[:, k, :], gat[:, ds(b * B, B)]))
                did.settle()
                dve.sem_inc(pidx_ready, 1)

            def new_features(b, k, half, ahead):
                dve.wait_ge(pg_full[k], 16 * B * half + 16 * B)
                xb = xs[:, ds(b * B, B), :]
                step(ve.tensor_tensor(xb, xb, pg[:, k, :, :], ALU.add))
                if ahead:
                    give_rows(b + 2, k)
                else:
                    dve.sem_inc(passed, 1)
                layer_statistics(b)
                did.settle()
                dve.sem_inc(var_ready, 1)

            def normaliser(b):
                dve.wait_ge(std_ready, b + 2)
                rb, nb = rstd[:, ds(b * B, B)], nmr[:, ds(b * B, B)]
                step(ve.reciprocal(rb, rb))
                ve.scalar_tensor_tensor(nb, mv[:, ds(b * B, B), 0], -1.0, rb, ALU.mult, ALU.mult).then_inc(ln_ready, 1)

            def split_tokens(b, k, i, first):
                dve.wait_ge(t_ready, b * B + B)
                if not first:
                    dve.wait_ge(scattered[k], 16 * 2 * B * i)
                xb = xs[:, ds(b * B, B), :]
                hi, lo = thl[:, k, :, 0:D], thl[:, k, :, D:2 * D]
                did.done(ve.tensor_copy(hi, t32))
                did.done(ve.tensor_tensor(xb, xb, t32, ALU.add))
                did.settle()
                step(ve.tensor_tensor(lo, t32, hi, ALU.subtract))

            def token_batch(b, k, i, first, more, ahead):
                def bc(a):
                    return a.unsqueeze(2).broadcast_to([P, B, E])

                split_tokens(b, k, i, first)
                if more:
                    new_features(b + 1, 1 - k, i + k, ahead)
                dve.wait_ge(lg_ready, b + 1)
                m, q, d, c1, c2 = (r7[:, n, :] for n in range(5))
                logit = bank[2][:, 0:B * E].rearrange("p (a e) -> p a e", e=E)
                step(ve.tensor_reduce(m, logit, AX.X, ALU.max))
                did.done(ve.tensor_tensor(lg, logit, bc(m), ALU.subtract))
                did.settle()
                dve.sem_inc(ldiff_ready, 1)
                if more:
                    normaliser(b + 1)
                dve.wait_ge(lexp_ready, b + 1)
                step(ve.tensor_reduce(q, lex, AX.X, ALU.add))
                step(ve.reciprocal(q, q))
                step(ve.tensor_tensor(pr, lex, bc(q), ALU.mult))
                rk = rank.unsqueeze(1).broadcast_to([P, B, E])

                def pick(top, hot):
                    step(ve.tensor_reduce(top, pr, AX.X, ALU.max))
                    step(ve.tensor_tensor(tmp, pr, bc(top), ALU.is_equal))
                    step(ve.tensor_tensor(tmp, tmp, rk, ALU.mult))
                    step(ve.tensor_reduce(q, tmp, AX.X, ALU.max))
                    step(ve.tensor_tensor(hot, rk, bc(q), ALU.is_equal))

                pick(c1, oh1)
                step(ve.scalar_tensor_tensor(pr, oh1, -2.0, pr, ALU.mult, ALU.add))
                pick(c2, oh2)
                step(ve.tensor_tensor(d, c1, c2, ALU.add))
                step(ve.tensor_scalar(d, d, 1e-12, None, ALU.max))
                step(ve.reciprocal(d, d))
                did.done(ve.tensor_tensor(comb[:, 0, ds(b * B, B)], c1, d, ALU.mult))
                did.done(ve.tensor_tensor(comb[:, 1, ds(b * B, B)], c2, d, ALU.mult))
                did.done(ve.tensor_tensor(msk[:, 0:B, :], oh1, oh2, ALU.add))
                did.settle()
                dve.sem_inc(msk_ready, 1)
                dve.wait_ge(pos_ready, b + 1)
                place = bank[3][:, 0:B * E].rearrange("p (a e) -> p a e", e=E)
                step(ve.tensor_tensor(pos, place, base8[:, :].unsqueeze(1).broadcast_to([P, B, E]), ALU.add))
                for r, hot in ((0, oh1), (1, oh2)):
                    step(ve.tensor_tensor(tmp, hot, pos, ALU.mult))
                    step(ve.tensor_reduce(c1 if r == 0 else c2, tmp, AX.X, ALU.add))
                for r, v in ((0, c1), (1, c2)):
                    did.done(ve.tensor_copy(sidx[:, k, r, :], v))
                    did.done(ve.tensor_copy(slots[:, r, ds(b * B, B)], v))
                did.done(ve.tensor_tensor(base8[:, :], base8[:, :], bank[3][:, B * E:(B + 1) * E], ALU.add))
                did.settle()
                dve.sem_inc(sidx_ready, 1)

            step(ve.tensor_copy(base8[:, :], eoff))
            give_rows(0, 0)
            give_rows(1, 1)
            new_features(0, 0, 0, True)
            normaliser(0)
            start3 = did.base + did.n
            did.start(start3)
            token_batch(0, 0, 0, True, True, True)
            PER3 = did.n
            did.start(start3 + PER3)
            token_batch(1, 1, 0, True, True, True)
            with dve.Fori(1, NB // 2 - 2) as i:
                for k in range(2):
                    did.start(start3 + (2 * i + k) * PER3)
                    token_batch(2 * i + k, k, i, False, True, True)
            did.start(start3 + (NB - 4) * PER3)
            token_batch(NB - 4, 0, NB // 2 - 2, False, True, True)
            token_batch(NB - 3, 1, NB // 2 - 2, False, True, False)
            token_batch(NB - 2, 0, NB // 2 - 1, False, True, False)
            token_batch(NB - 1, 1, NB // 2 - 1, False, False, False)

            step(ve.tensor_copy(zrow[:, :], base8[:, :]))
            dve.sem_inc(zrow_ready, 1)
            step(ve.tensor_tensor(cnt[:, :], base8[:, :], eoff, ALU.subtract))
            step(ve.tensor_scalar(nt8, cnt[:, :], float(XT - 1), None, ALU.add))
            step(ve.tensor_scalar(nt8, nt8, 8, None, ALU.logical_shift_right))
            step(ve.tensor_copy(ntf, nt8))
            step(ve.tensor_tensor_scan(cend, ntf, zero8, 0.0, ALU.add, ALU.add))
            step(ve.tensor_copy(cnt[:, :], cend))
            step(ve.tensor_copy(base8[:, :], ntf))
            step(ve.tensor_tensor_scan(jidx, one8[:, :].broadcast_to([P, NT]), zcol[:, :].broadcast_to([P, NT]), -1.0, ALU.add,
                                       ALU.add))
            step(ve.tensor_tensor(tge, cnt[:, :].unsqueeze(1).broadcast_to([P, NT, E]),
                                  jidx.unsqueeze(2).broadcast_to([P, NT, E]), ALU.is_le))
            step(ve.tensor_reduce(tej, tge, AX.X, ALU.add))
            step(ve.tensor_tensor(tge, tge, base8[:, :].unsqueeze(1).broadcast_to([P, NT, E]), ALU.mult))
            step(ve.tensor_reduce(tst, tge, AX.X, ALU.add))
            step(ve.tensor_tensor(tst, jidx, tst, ALU.subtract))
            step(ve.tensor_scalar(tst, tst, float(XT), None, ALU.mult))
            step(ve.scalar_tensor_tensor(tab[:, 1, :], tej, float(R), tst, ALU.mult, ALU.add))
            step(ve.tensor_scalar(tab[:, 0, :], tej, float(E - 1), None, ALU.min))
            dve.sem_inc(tab_ready, 1)
            step(ve.tensor_tensor(start, cnt[:, :], base8[:, :], ALU.subtract))
            step(ve.tensor_scalar(start, start, float(XT), None, ALU.mult))
            row = slots[:, :, :].rearrange("p r t -> p (r t)")
            step(ve.tensor_scalar(which, row, RB, None, ALU.logical_shift_right))
            step(ve.tensor_scalar(whichf, which, -1.0, float(E), ALU.mult, ALU.add))
            step(ve.tensor_scalar(row, row, R - 1, None, ALU.bitwise_and))
            step(ve.tensor_tensor(chosen, whichf.unsqueeze(2).broadcast_to([P, 2 * T, E]),
                                  rank.unsqueeze(1).broadcast_to([P, 2 * T, E]), ALU.is_equal))
            step(ve.tensor_tensor(chosen, chosen, start.unsqueeze(1).broadcast_to([P, 2 * T, E]), ALU.mult))
            step(ve.tensor_reduce(whichf, chosen, AX.X, ALU.add))
            step(ve.tensor_tensor(row, row, whichf, ALU.add))
            end4 = did.base + did.n

            def take_tokens(j, k, first):
                dve.wait_ge(xt4_ready, j + 1)
                if not first:
                    dve.wait_ge(h_ready, j - 1)
                ve.tensor_copy(xT[:, k, 1, :, :].rearrange("p a b -> p (a b)"),
                               bank[6 + k][:, :].bitcast(f16)[:, 0:2 * XT]).then_inc(xt4_lo, 1)

            def split_hidden(j, k, first):
                dve.wait_ge(gelu_ready, j + 1)
                if not first:
                    dve.wait_ge(y_ready, j - 1)
                ve.tensor_copy(hh[:, k, :, :], h32[:, k, :, :]).then_inc(hh_ready, 1)
                dve.wait_ge(hh_ready, j + 1)
                ve.tensor_tensor(hl[:, k, :, :], h32[:, k, :, :], hh[:, k, :, :], ALU.subtract).then_inc(hl_ready, 1)

            def take_results(i, j, k, first):
                e = dve.value_load(tab[0:1, 0, ds(j, 1)], min_val=0, max_val=E - 1)
                dve.wait_ge(y_ready, j + 1)
                if not first:
                    dve.wait_ge(y_stored[k], 16 * i)
                bias = b2s[:, ds(e, 1), :].broadcast_to([P, 2, D])
                ve.scalar_tensor_tensor(yb[:, k, :, :], bank[4 + k][:, :].rearrange("p (h d) -> p h d", h=2),
                                        1.0 / SCALE, bias, ALU.mult, ALU.add).then_inc(y_taken, 1)

            def step_of_two(i, first):
                for k in range(2):
                    j = 2 * i + k
                    take_tokens(j + 2, k, False)
                    split_hidden(j + 1, 1 - k, first and k == 0)
                    take_results(i, j, k, first)

            take_tokens(0, 0, True)
            take_tokens(1, 1, True)
            split_hidden(0, 0, True)
            dve.wait_ge(s_b2, 16)
            step_of_two(0, True)
            with dve.Fori(1, NT // 2 - 1) as i:
                step_of_two(i, False)
            split_hidden(NT - 1, 1, False)
            take_results(NT // 2 - 1, NT - 2, 0, False)
            take_results(NT // 2 - 1, NT - 1, 1, False)


            def give_slots(b, k, base):
                did.start(base)
                did.done(ve.tensor_copy(yidx[:, k, :, :], slots[:, :, ds(b * B, B)]))
                did.settle()
                dve.sem_inc(yidx_ready, 1)

            def result_batch(b, k, i, ahead, base):
                did.start(base)
                dve.wait_ge(yg_full[k], 16 * 2 * B * i + 16 * 2 * B)
                for r in range(2):
                    for s in range(B):
                        t = b * B + s
                        xt_ = xs[:, ds(t, 1), :].rearrange("p a d -> p (a d)")
                        did.done(ve.scalar_tensor_tensor(xt_, yg[:, k, r, s, :], comb[:, r, ds(t, 1)], xt_, ALU.mult,
                                                         ALU.add))
                    did.settle()
                dve.sem_inc(out_ready, 1)
                if ahead:
                    give_slots(b + 2, k, base + 2 * B)

            give_slots(0, 0, end4)
            give_slots(1, 1, end4 + 1)
            start5 = end4 + 2
            with dve.Fori(0, NB // 2 - 1) as i:
                for k in range(2):
                    result_batch(2 * i + k, k, i, True, start5 + (2 * i + k) * (2 * B + 1))
            for k in range(2):
                result_batch(NB - 2 + k, k, NB // 2 - 1, False, start5 + (NB - 2) * (2 * B + 1) + k * 2 * B)


def kernel(x, src, dst, L0_gnn_W, L0_gnn_b, L0_ffn_router_w, L0_ffn_w1, L0_ffn_b1, L0_ffn_w2, L0_ffn_b2):
    import numpy as np
    import concourse.bacc as bacc
    from concourse import mybir as mb
    from concourse.bass_utils import run_bass_kernel_spmd

    src, dst = np.asarray(src), np.asarray(dst)
    s, d = src.reshape(NCH, CH), dst.reshape(NCH, CH)
    arrays = {
        "x": np.asarray(x),
        "src_cols": s.T,
        "edge_rows": np.concatenate([s, d], axis=1),
        "wg": np.asarray(L0_gnn_W).reshape(D, 2, 2, P).transpose(3, 2, 1, 0).reshape(P, 4 * D),
        "bg": np.asarray(L0_gnn_b),
        "rw": np.asarray(L0_ffn_router_w).reshape(E, 2, P).transpose(2, 1, 0).reshape(P, 2 * E),
        "w1": np.asarray(L0_ffn_w1),
        "b1": np.asarray(L0_ffn_b1).reshape(E, 2, P).transpose(2, 0, 1).reshape(P, 2 * E),
        "w2": np.asarray(L0_ffn_w2),
        "b2": np.asarray(L0_ffn_b2),
    }
    arrays = {k: np.ascontiguousarray(v) for k, v in arrays.items()}
    nc = bacc.Bacc("TRN2", target_bir_lowering=False, num_devices=1)
    args = [nc.dram_tensor(k, v.shape, mb.dt.from_np(v.dtype), kind="ExternalInput").ap() for k, v in arrays.items()]
    out = nc.dram_tensor("out", (N, D), mb.dt.float32, kind="ExternalOutput").ap()
    gnn_moe(nc, *args, out)
    return run_bass_kernel_spmd(nc, [arrays], core_ids=[0]).results[0]["out"]
```
